# Optimizing a Trainium2 kernel written in Bass

```python
import numpy as np
import jax
import jax.numpy as jnp

def _softmax(x, axis=-1):
    return jax.nn.softmax(x, axis=axis)

def _gelu(x):
    return jax.nn.gelu(x, approximate=True)

def _silu(x):
    return jax.nn.silu(x)

def _sigmoid(x):
    return jax.nn.sigmoid(x)

def _layernorm(x, axis=-1, eps=1e-05):
    m = jnp.mean(x, axis=axis, keepdims=True)
    v = jnp.var(x, axis=axis, keepdims=True)
    return (x - m) / jnp.sqrt(v + eps)

def _scatter_add(tgt, idx, src, axis=0):
    return tgt.at[idx].add(src)

def _segment_sum(src, seg, n):
    return jax.ops.segment_sum(src, seg, n)
kernel_name = 'mk_flamingo_gated_d1_seqx_r2_763abb'

def setup_inputs(seed: int=0):
    np.random.seed(seed)
    _w = jnp.asarray

    def _rec_inputs():
        import jax
        import jax.numpy as jnp
        _rk = jax.random.key(seed)
        x = -0.0003929 + 0.9999 * jax.random.normal(jax.random.fold_in(_rk, 1), (16, 256, 2048), jnp.float32)
        _lenS = 256 - jax.random.randint(jax.random.fold_in(_rk, 7), (16,), 0, max(1, 256 // 4) + 1, jnp.int32)
        _lenS2 = 256 - jax.random.randint(jax.random.fold_in(_rk, 8), (16,), 0, max(1, 256 // 4) + 1, jnp.int32)
        _ctx_1024P = jax.random.normal(jax.random.fold_in(_rk, 11), (16, 16, 512), jnp.float32)
        _ctx_1024c = jax.random.dirichlet(jax.random.fold_in(_rk, 511), 0.3 * jnp.ones((16,), jnp.float32), (16, 256))
        _ctx_1024t = jnp.einsum('bsk,bkd->bsd', _ctx_1024c, _ctx_1024P)
        _ctx_1024t = _ctx_1024t * jax.lax.rsqrt(jnp.mean(jnp.square(_ctx_1024t)) + 1e-12) * 0.953939
        ctx_1024 = -1.39393e-06 + 0.999914 * (_ctx_1024t + 0.3 * jax.random.normal(jax.random.fold_in(_rk, 611), (16, 256, 512), jnp.float32))
        _g = jax.random.normal(jax.random.fold_in(_rk, 9001), (2, 1), jnp.float32)
        _g = jnp.sign(_g) * jnp.maximum(jnp.abs(_g), 1.0) + (_g == 0) * 1.0
        g_xattn = _g[0]
        g_ffn = _g[1]
        return (x, ctx_1024, g_xattn, g_ffn)
    x, ctx_1024, g_xattn, g_ffn = _rec_inputs()

    def _L0_xattn_setup():
        import jax, jax.numpy as jnp
        import numpy as np
        import math
        DIM_V = 256
        key = jax.random.key(seed)
        k1, k2, k3, k4, k5, k6 = jax.random.split(key, 6)
        B, C, N, M = (8, DIM_V, 2048, 512)
        pcd_up = jax.random.normal(k1, (B, C, N), dtype=jnp.float32)
        pcd_down = jax.random.normal(k2, (B, C, M), dtype=jnp.float32)
        s = 1.0 / math.sqrt(C)
        Wq = jax.random.normal(k3, (C, C), dtype=jnp.float32) * s
        Wk = jax.random.normal(k4, (C, C), dtype=jnp.float32) * s
        Wv = jax.random.normal(k5, (C, C), dtype=jnp.float32) * s
        Wskip = jax.random.normal(k6, (C, C), dtype=jnp.float32) * s
        return {'pcd_up': pcd_up, 'pcd_down': pcd_down, 'Wq': Wq, 'Wk': Wk, 'Wv': Wv, 'Wskip': Wskip}
    _L0_xattn_all = _L0_xattn_setup()
    _L0_xattn_in = {k: v for k, v in _L0_xattn_all.items() if k in ('Wq', 'Wk', 'Wv', 'Wskip')}
    del _L0_xattn_all

    def _L0_ffn_setup():
        import jax, jax.numpy as jnp
        import numpy as np
        B_, S, D_IN, D_OUT = (4, 1024, 2048, 2048)
        N, RANK, ALPHA = (8, 16, 32)
        SCALE = ALPHA / RANK
        key = jax.random.key(seed)
        kx, ka, kb, kw, kbias = jax.random.split(key, 5)
        x = jax.random.normal(kx, (B_, S, D_IN), dtype=jnp.float32)
        lora_A = jax.random.normal(ka, (N, RANK, D_IN), dtype=jnp.float32) * (1.0 / np.sqrt(D_IN))
        lora_B = jax.random.normal(kb, (N, D_OUT, RANK), dtype=jnp.float32) * (1.0 / np.sqrt(RANK))
        W = jax.random.normal(kw, (D_OUT, D_IN), dtype=jnp.float32) * (1.0 / np.sqrt(D_IN))
        bias = jax.random.normal(kbias, (D_OUT,), dtype=jnp.float32) * 0.01
        lora_weights = jnp.full((N,), 1.0 / N, dtype=jnp.float32)
        return {'x': x, 'lora_A': lora_A, 'lora_B': lora_B, 'W': W, 'bias': bias, 'lora_weights': lora_weights}
    _L0_ffn_all = _L0_ffn_setup()
    _L0_ffn_in = {k: v for k, v in _L0_ffn_all.items() if k in ('lora_A', 'lora_B', 'W', 'bias', 'lora_weights')}
    del _L0_ffn_all
    return {'x': x, 'ctx_1024': ctx_1024, 'g_xattn': g_xattn, 'g_ffn': g_ffn, 'L0_xattn_Wq': _L0_xattn_in['Wq'], 'L0_xattn_Wk': _L0_xattn_in['Wk'], 'L0_xattn_Wv': _L0_xattn_in['Wv'], 'L0_xattn_Wskip': _L0_xattn_in['Wskip'], 'L0_ffn_lora_A': _L0_ffn_in['lora_A'], 'L0_ffn_lora_B': _L0_ffn_in['lora_B'], 'L0_ffn_W': _L0_ffn_in['W'], 'L0_ffn_bias': _L0_ffn_in['bias'], 'L0_ffn_lora_weights': _L0_ffn_in['lora_weights']}

def reference(x, ctx_1024, g_xattn, g_ffn, L0_xattn_Wq, L0_xattn_Wk, L0_xattn_Wv, L0_xattn_Wskip, L0_ffn_lora_A, L0_ffn_lora_B, L0_ffn_W, L0_ffn_bias, L0_ffn_lora_weights):
    import jax
    import jax.numpy as jnp

    def _L0_xattn_ref(pcd_up, pcd_down, Wq, Wk, Wv, Wskip):
        import jax, jax.numpy as jnp
        import numpy as np
        import math
        DIM_V = 256
        q = jnp.einsum('oc,bcn->bon', Wq, pcd_up)
        k = jnp.einsum('oc,bcm->bom', Wk, pcd_down)
        v = jnp.einsum('oc,bcm->bom', Wv, pcd_down)
        C = q.shape[1]
        scale = jnp.sqrt(jnp.asarray(C, dtype=q.dtype))
        energy = jnp.einsum('bcn,bcm->bnm', q, k) / scale
        attention = jax.nn.softmax(energy, axis=-1)
        x = jnp.einsum('bnm,bcm->bcn', attention, v)
        skip = jnp.einsum('oc,bcn->bon', Wskip, pcd_up)
        return skip + x

    def _L0_ffn_ref(x, lora_A, lora_B, W, bias, lora_weights):
        import jax, jax.numpy as jnp
        import numpy as np
        B_, S, D_IN, D_OUT = (4, 1024, 2048, 2048)
        N, RANK, ALPHA = (8, 16, 32)
        SCALE = ALPHA / RANK
        h = jnp.einsum('bsd,nrd->nbsr', x, lora_A)
        coef = (SCALE * lora_weights)[:, None, None]
        lora_out = jnp.einsum('nbsr,nor->bso', h, lora_B * coef)
        base = jnp.einsum('bsd,od->bso', x, W) + bias
        return base + lora_out
    x = x + jnp.tanh(g_xattn[0]) * _L0_xattn_ref(_layernorm(x, axis=-1), ctx_1024, L0_xattn_Wq, L0_xattn_Wk, L0_xattn_Wv, L0_xattn_Wskip)
    x = x + jnp.tanh(g_ffn[0]) * _L0_ffn_ref(_layernorm(x, axis=-1), L0_ffn_lora_A, L0_ffn_lora_B, L0_ffn_W, L0_ffn_bias, L0_ffn_lora_weights)
    return x

_drawn_inputs = setup_inputs


def setup_inputs(seed=0):
    import zlib

    import numpy as np

    out = dict(_drawn_inputs(seed))
    spreads = {'L0_ffn_lora_weights': (0.125, 0.2)}
    factors = {'L0_ffn_bias': 8.0}
    for name, (base, spread) in spreads.items():
        noise = np.random.default_rng([zlib.crc32(name.encode()), seed]).standard_normal(out[name].shape)
        drawn = base * np.exp(spread * noise) if base else spread * noise
        out[name] = jnp.asarray(drawn.astype(out[name].dtype))
    for name, factor in factors.items():
        out[name] = (out[name] * factor).astype(out[name].dtype)
    return out
```

```python
from contextlib import ExitStack

import concourse.bass as bass
from concourse import mybir

F32 = mybir.dt.float32
F16 = mybir.dt.float16
U32 = mybir.dt.uint32
ALU = mybir.AluOpType
ACT = mybir.ActivationFunctionType
AX = mybir.AxisListType
RMAX = bass.bass_isa.ReduceOp.max

P = 128
EXPONENT = 0x7F800000
TINY = 1e-30
EPS = 1e-5
U_EXP = 10
P_EXP = 14
IN_EXP = 6
GV_EXP = -7
W_EXP = 14
LORA_SCALE = 2.0


def flamingo_kernel(nc, x, ctx_in, g_xattn, g_ffn, wq, wk, wv, wskip, lora_a, lora_b, w, bias,
                    lora_weights, out):
    B, C, N = x.shape
    M = ctx_in.shape[2]
    NADAPT, RANK, D = lora_a.shape
    O = w.shape[0]
    CT = C // P
    MT = M // P
    CH = 512
    NQ = N // CH
    TPC = CH // P
    TPB = N // P
    KT = D // P
    OC = O // CH
    ST = B * C // P
    PPB = 2 * CT * NQ // CT + 2
    assert CT == 2 and MT == 4 and NQ == 4 and TPC == 4 and NADAPT * RANK == P and PPB == 10

    x1_dram = nc.dram_tensor("x1_scratch", [B, C, N], F32, kind="Internal").ap()
    x_rows = x.rearrange("b (t p) n -> b p t n", p=P)
    x1_rows = x1_dram.rearrange("b (t p) n -> b p t n", p=P)
    x1_tiles = x1_dram.rearrange("b (t p) n -> (b t) p n", p=P)
    out_tiles = out.rearrange("b (t p) n -> (b t) p n", p=P)
    ctx_rows = ctx_in.rearrange("b (t p) m -> b p t m", p=P)

    with ExitStack() as outer:
        def sem(name):
            return outer.enter_context(nc.semaphore(name))

        def keep(name, shape, dt):
            return outer.enter_context(nc.sbuf_tensor(name, shape, dt))

        ident = keep("ident", [P, P], F32)
        xring = keep("xring", [P, 4, D], F32)
        u2 = keep("u2", [P, D], F32)
        bt = keep("bt", [P, O], F32)
        biasg = keep("biasg", [P, O], F32)
        tg = keep("tg", [P, 2], F32)
        coef = keep("coef", [P, 1], F32)
        wabs = keep("wabs", [P, O * D // (P * 1024)], F32)
        minus_half = keep("minus_half", [P, 2], F32)
        idle_pool = keep("idle_pool", [P, 1], F32)
        idle_dve = keep("idle_dve", [P, 1], F32)
        a_nat = xring[:, 1, :]
        w_stage = [xring[:, 2 + i, :].rearrange("p (t d) -> p t d", t=4) for i in range(2)]
        b_nat = u2[:, :].rearrange("p (t n r) -> p t n r", n=NADAPT, r=RANK)

        s_ident0 = sem("s_ident0")
        s_ident = sem("s_ident")
        s_lora_in = sem("s_lora_in")
        s_wstage = [sem("s_wstage0"), sem("s_wstage1")]

        def load_w_block(eng, blk):
            oc, db = blk // 4, blk % 4
            src = w[oc * CH:(oc + 1) * CH, db * 512:(db + 1) * 512].rearrange("(t p) d -> p t d", p=P)
            eng.dma_start(w_stage[blk % 2], src).then_inc(s_wstage[blk % 2], 16)

        with ExitStack() as phase:
            def sb(name, shape, dt):
                return phase.enter_context(nc.sbuf_tensor(name, shape, dt))

            def ps(name):
                return phase.enter_context(nc.psum_tensor(name, [P, CH], F32))

            xb = sb("xb", [P, 2, CT, N], F32)
            uh = sb("uh", [P, CT, N], F16)
            ul = sb("ul", [P, CT, N], F16)
            u32 = sb("u32", [P, CT, CH], F32)
            pf = sb("pf", [P, 4, M], F32)
            pth = sb("pth", [P, 2, MT, CH], F16)
            ptl = sb("ptl", [P, 2, MT, CH], F16)
            ctxr = sb("ctxr", [P, CT, M], F32)
            ctxh = sb("ctxh", [P, CT, M], F16)
            ctxl = sb("ctxl", [P, CT, M], F16)
            gh = sb("gh", [P, 2, CT, M], F16)
            gl = sb("gl", [P, 2, CT, M], F16)
            vh = sb("vh", [P, 2, MT, C], F16)
            vl = sb("vl", [P, 2, MT, C], F16)
            w_nat = sb("w_nat", [P, 4, CT, C], F32)
            wt32 = sb("wt32", [P, 3, CT, C], F32)
            wth = sb("wth", [P, 3, CT, C], F16)
            wtl = sb("wtl", [P, 3, CT, C], F16)
            wscan = sb("wscan", [P, 2, 1024], F32)
            wjunk = sb("wjunk", [P, 1024], F32)
            gates = sb("gates", [P, 2], F32)
            wmax = sb("wmax", [P, 3], F32)
            wmaxa = sb("wmaxa", [P, 3], F32)
            wpow = sb("wpow", [P, 3], F32)
            wrec = sb("wrec", [P, 3], F32)
            wscale = sb("wscale", [P, 3], F32)
            c_exp = sb("c_exp", [P, 1], F32)
            c_att = sb("c_att", [P, 1], F32)
            a_skip = sb("a_skip", [P, 1], F32)
            cmax = sb("cmax", [P, 1], F32)
            cmaxa = sb("cmaxa", [P, 1], F32)
            cpow = sb("cpow", [P, 1], F32)
            crec = sb("crec", [P, 1], F32)
            cscale = sb("cscale", [P, 1], F32)
            e_scale = sb("e_scale", [P, 2], F32)
            a_att = sb("a_att", [P, 2], F32)
            nmax = sb("nmax", [P, 4], F32)
            nbias = sb("nbias", [P, 4], F32)
            rsum = sb("rsum", [P, 4], F32)
            rinv = sb("rinv", [P, 4], F32)
            stats = sb("stats", [P, CT, NQ, 6], F32)
            mv = sb("mv", [P, CT, 2], F32)
            vare = sb("vare", [P, CT], F32)
            rstd = sb("rstd", [P, 2, CT], F32)
            mean = sb("mean", [P, 2, CT], F32)

            ps_e = [ps("ps_e0"), ps("ps_e1")]
            ps_t = [ps("ps_t0"), ps("ps_t1")]
            ps_p = [[ps("ps_p00"), ps("ps_p01")], [ps("ps_p10"), ps("ps_p11")]]

            s_w_in = sem("s_w_in")
            s_gates_in = sem("s_gates_in")
            s_tanh = sem("s_tanh")
            s_half = sem("s_half")
            s_biasg = sem("s_biasg")
            s_bias_in = sem("s_bias_in")
            s_wt_ps = sem("s_wt_ps")
            s_wt32 = sem("s_wt32")
            s_wmax = sem("s_wmax")
            s_wmaxa = sem("s_wmaxa")
            s_wsc = sem("s_wsc")
            s_wth = sem("s_wth")
            s_wtl = sem("s_wtl")
            s_x_in = [sem("s_x_in0"), sem("s_x_in1")]
            s_ctx_in = sem("s_ctx_in")
            s_x1_stored = sem("s_x1_stored")
            s_scan_in = [sem("s_scan_in0"), sem("s_scan_in1")]
            s_scanned = sem("s_scanned")
            s_stats = sem("s_stats")
            s_aggr = sem("s_aggr")
            s_vare = sem("s_vare")
            s_rstd = sem("s_rstd")
            s_u32 = sem("s_u32")
            s_uh = sem("s_uh")
            s_ul = sem("s_ul")
            s_cmax = sem("s_cmax")
            s_cmaxa = sem("s_cmaxa")
            s_csc = sem("s_csc")
            s_ctxh = sem("s_ctxh")
            s_ctxl = sem("s_ctxl")
            s_gvh = sem("s_gvh")
            s_gv = sem("s_gv")
            s_energy = sem("s_energy")
            s_nmax = sem("s_nmax")
            s_nbias = sem("s_nbias")
            s_exp = sem("s_exp")
            s_rinv = sem("s_rinv")
            s_pn = sem("s_pn")
            s_t = sem("s_t")
            s_pth = sem("s_pth")
            s_ptl = sem("s_ptl")
            s_pair = sem("s_pair")
            s_escale = sem("s_escale")
            s_mean = sem("s_mean")
            s_skip_add = sem("s_skip_add")
            s_x1 = sem("s_x1")

            SCANS = O * D // (P * 1024)
            SPB = SCANS // B
            assert SPB == 2
            w_pieces = w.rearrange("o (h d) -> (o h) d", d=1024).rearrange("(n p) d -> n p d", p=P)

            OLD = {0: (2, 1, -1), 3: (3, 0, 0), 4: (3, 1, 1)}
            OWN = {7: (0, 0, 2), 8: (0, 1, 3), 11: (1, 0, 6), 12: (1, 1, 7), 15: (2, 0, 8)}
            GV = {9: (0, 4), 10: (1, 5)}
            BANK = {0: 1, 3: 0, 4: 1, 7: 0, 8: 1, 9: 0, 10: 1, 11: 0, 12: 1, 15: 0}

            def attention_pair(b, par, s, first, last):
                if s in OLD and not first:
                    q, ct, n = OLD[s]
                    return b - 1, 1 - par, q, ct, PPB * b + n, BANK[s]
                if s in OWN:
                    q, ct, n = OWN[s]
                    return b, par, q, ct, PPB * b + n - (2 if last and n > 5 else 0), BANK[s]
                return None

            def tail_pair(s):
                q, ct, n = OLD[s]
                return B - 1, (B - 1) % 2, q, ct, PPB * B + n - 2, BANK[s]

            def batches(emit, eng):
                emit(0, 0, True, False)
                with eng.Fori(0, (B - 2) // 2) as i:
                    emit(2 * i + 1, 1, False, False)
                    emit(2 * i + 2, 0, False, False)
                emit(B - 1, (B - 1) % 2, False, True)

            with nc.Block() as block:

                @block.sync
                def _(sp):
                    def store_x1(b, par, q, ct, n):
                        sp.wait_ge(s_x1, n + 1)
                        sp.dma_start(x1_rows[b, :, ct, q * CH:(q + 1) * CH],
                                     xb[:, par, ct, q * CH:(q + 1) * CH]).then_inc(s_x1_stored, 16)

                    def load_x(b, par):
                        for ct in range(CT):
                            sp.dma_start(xb[:, par, ct, :], x_rows[b, :, ct, :]).then_inc(s_x_in[par], 16)

                    for i, t in enumerate((wq, wk, wv, wskip)):
                        sp.dma_start(w_nat[:, i, :, :], t.rearrange("(t p) c -> p t c", p=P)).then_inc(s_w_in, 16)
                    sp.dma_start(ctxr[:, :, :], ctx_rows[0, :, :, :]).then_inc(s_ctx_in, 16)
                    load_x(0, 0)
                    sp.dma_start(gates[:, 0:1], g_xattn.rearrange("(a n) -> a n", a=1).to_broadcast([P, 1])
                                 ).then_inc(s_gates_in, 16)
                    sp.dma_start(gates[:, 1:2], g_ffn.rearrange("(a n) -> a n", a=1).to_broadcast([P, 1])
                                 ).then_inc(s_gates_in, 16)
                    sp.dma_start(biasg[:, :], bias.rearrange("(a n) -> a n", a=1).to_broadcast([P, O])
                                 ).then_inc(s_bias_in, 16)

                    sp.dma_start(a_nat, lora_a.rearrange("n r d -> (n r) d")).then_inc(s_lora_in, 16)
                    for n in range(NADAPT):
                        sp.dma_start(coef[n * RANK:(n + 1) * RANK, :],
                                     lora_weights[n:n + 1].rearrange("(a n) -> a n", a=1).to_broadcast([RANK, 1])
                                     ).then_inc(s_lora_in, 16)
                    load_w_block(sp, 0)
                    load_w_block(sp, 1)
                    for n in range(NADAPT):
                        sp.dma_start(b_nat[:, :, n, :], lora_b[n].rearrange("(p t) r -> p t r", p=P)
                                     ).then_inc(s_lora_in, 16)

                    def emit(b, par, first, last):
                        if not last:
                            sp.wait_ge(s_ctxl, b + 1)
                            sp.dma_start(ctxr[:, :, :], ctx_rows[b + 1, :, :, :]).then_inc(s_ctx_in, 16)
                        if not first:
                            store_x1(b - 1, 1 - par, 2, 0, 8 * b - 4)
                            store_x1(b - 1, 1 - par, 2, 1, 8 * b - 3)
                            store_x1(b - 1, 1 - par, 3, 0, 8 * b - 2)
                            store_x1(b - 1, 1 - par, 3, 1, 8 * b - 1)
                            sp.wait_ge(s_x1_stored, 16 * 8 * b)
                        if not last:
                            load_x(b + 1, 1 - par)
                        for q in range(2):
                            store_x1(b, par, q, 0, 8 * b + 2 * q)
                            store_x1(b, par, q, 1, 8 * b + 2 * q + 1)


                    batches(emit, sp)
                    n = 8 * B - 4
                    for q in (2, 3):
                        for ct in range(CT):
                            store_x1(B - 1, (B - 1) % 2, q, ct, n)
                            n += 1
                    sp.wait_ge(s_x1_stored, 16 * 8 * B)

                @block.gpsimd
                def _(pool):
                    nc.gpsimd.memset(ident[:, :], 0.0).then_inc(s_ident0, 1)
                    nc.gpsimd.memset(minus_half[:, :], -0.5).then_inc(s_half, 1)
                    pool.wait_ge(s_ident0, 1)
                    nc.gpsimd.affine_select(out=ident[:, :], in_=ident[:, :], compare_op=ALU.not_equal, fill=1.0,
                                            base=0, pattern=[[-1, P]], channel_multiplier=1).then_inc(s_ident, 1)
                    def rstd_of(b, par):
                        pool.wait_ge(s_vare, b + 1)
                        nc.gpsimd.tensor_tensor(rstd[:, par, :], vare[:, :], minus_half[:, 0:CT],
                                                ALU.pow).then_inc(s_rstd, 1)

                    def u_low(b, q):
                        for ct in range(CT):
                            pool.wait_ge(s_uh, 8 * b + 2 * q + ct + 1)
                            cols = slice(q * CH, (q + 1) * CH)
                            nc.gpsimd.tensor_tensor(ul[:, ct, cols], u32[:, ct, :], uh[:, ct, cols],
                                                    ALU.subtract).then_inc(s_ul, 1)

                    def ctx_max(b):
                        pool.wait_ge(s_cmax, b + 1)
                        nc.gpsimd.tensor_tensor(idle_pool[:, :], minus_half[:, 0:1], minus_half[:, 1:2], ALU.add)
                        nc.gpsimd.partition_all_reduce(cmaxa[:, :], cmax[:, :], P, RMAX).then_inc(s_cmaxa, 1)

                    pool.wait_ge(s_half, 1)
                    ctx_max(0)
                    rstd_of(0, 0)
                    pool.wait_ge(s_wmax, 3)
                    nc.gpsimd.partition_all_reduce(wmaxa[:, :], wmax[:, :], P, RMAX).then_inc(s_wmaxa, 1)
                    u_low(0, 0)
                    u_low(0, 1)

                    def emit(b, par, first, last):
                        if not last:
                            ctx_max(b + 1)
                        u_low(b, 2)
                        u_low(b, 3)
                        if not last:
                            rstd_of(b + 1, 1 - par)
                            u_low(b + 1, 0)
                            u_low(b + 1, 1)

                    batches(emit, pool)

                @block.scalar
                def _(act):
                    act.wait_ge(s_gates_in, 32)
                    nc.scalar.activation(tg[:, :], gates[:, :], ACT.Tanh).then_inc(s_tanh, 1)

                    def ctx_high(b):
                        act.wait_ge(s_csc, 4 * b + 4)
                        nc.scalar.activation(ctxh[:, :, :], ctxr[:, :, :], ACT.Copy,
                                             scale=cscale[:, 0:1]).then_inc(s_ctxh, 1)

                    def gv_high(b, par, which, n):
                        act.wait_ge(s_pair, n + 1)
                        for k in range(2):
                            dst = gh[:, par, k, :] if which == 0 else \
                                vh[:, par, 2 * k:2 * k + 2, :].rearrange("p t c -> p (t c)")
                            nc.scalar.activation(dst, ps_p[which][k][:, :], ACT.Copy,
                                                 scale=2.0 ** GV_EXP).then_inc(s_gvh, 1)

                    def u_high(b, q, free):
                        if free is not None:
                            act.wait_ge(s_pair, free)
                        for ct in range(CT):
                            act.wait_ge(s_u32, 8 * b + 2 * q + ct + 1)
                            nc.scalar.activation(uh[:, ct, q * CH:(q + 1) * CH], u32[:, ct, :],
                                                 ACT.Copy).then_inc(s_uh, 1)

                    ctx_high(0)
                    act.wait_ge(s_wsc, 4)
                    for i in range(3):
                        nc.scalar.activation(wth[:, i, :, :], wt32[:, i, :, :], ACT.Copy,
                                             scale=wscale[:, i:i + 1]).then_inc(s_wth, 1)
                    u_high(0, 0, None)
                    gv_high(0, 0, 0, 0)
                    gv_high(0, 0, 1, 1)
                    u_high(0, 1, None)

                    def exp_tile(b, par, s, first):
                        j = TPB * b + s
                        act.wait_ge(s_nbias, j + 1)
                        if not (first and s < 4):
                            act.wait_ge(s_t, j - 3)
                        nc.scalar.activation(pf[:, s % 4, :], ps_e[s % 2][:, :], ACT.Exp,
                                             bias=nbias[:, s % 4:s % 4 + 1], scale=e_scale[:, par:par + 1],
                                             accum_out=rsum[:, s % 4:s % 4 + 1]).then_inc(s_exp, 1)

                    def p_high(j, s):
                        act.wait_ge(s_t, j + 1)
                        nc.scalar.activation(pth[:, (s // TPC) % 2, :, (s % TPC) * P:(s % TPC + 1) * P],
                                             ps_t[s % 2][:, :].rearrange("p (t n) -> p t n", t=MT),
                                             ACT.Copy).then_inc(s_pth, 1)

                    def load_piece(n, i):
                        act.dma_start(wscan[:, i, :], w_pieces[n, :, :]).then_inc(s_scan_in[i], 16)

                    def scan(b, i, final):
                        n = SPB * b + i
                        if not final:
                            if not (isinstance(n, int) and n == 0):
                                act.wait_ge(s_scanned, n)
                            load_piece(n + 1, 1 - i)
                        act.wait_ge(s_scan_in[i], 16 * (b + 1))
                        nc.scalar.activation(wjunk[:, :], wscan[:, i, :], ACT.Abs,
                                             accum_out=wabs[:, bass.ds(n, 1)]).then_inc(s_scanned, 1)

                    load_piece(0, 0)

                    def emit(b, par, first, last):
                        for s in range(TPB):
                            exp_tile(b, par, s, first)
                            if not (first and s < 2):
                                p_high(TPB * b + s - 2, (s - 2) % TPB)
                            if s == 2:
                                u_high(b, 2, None if first else PPB * b)
                            if s == 6:
                                u_high(b, 3, None if first else PPB * b + 2)
                            if not last and s == 7:
                                ctx_high(b + 1)
                            if not last and s - 1 in GV:
                                which, n = GV[s - 1]
                                gv_high(b + 1, 1 - par, which, PPB * b + n)
                            if not last and s == 13:
                                u_high(b + 1, 0, PPB * b + 4)
                            if not last and s == 15:
                                u_high(b + 1, 1, PPB * b + 8)
                            if s in (5, 14):
                                scan(b, 0 if s == 5 else 1, last and s == 14)

                    batches(emit, act)
                    for s in (TPB - 2, TPB - 1):
                        p_high(TPB * (B - 1) + s, s)

                @block.vector
                def _(dve):
                    def stats_of(b, par, parts):
                        for part in parts:
                            ct, q = part // NQ, part % NQ
                            if q == 0:
                                dve.wait_ge(s_x_in[par], 16 * (b - par) + 32)
                            nc.vector.bn_stats(stats[:, ct, q, :], xb[:, par, ct, q * CH:(q + 1) * CH]
                                               ).then_inc(s_stats, 1)

                    def aggregate(b, par):
                        dve.wait_ge(s_stats, 8 * (b + 1))
                        nc.vector.tensor_copy(idle_dve[:, :], minus_half[:, 0:1])
                        for ct in range(CT):
                            nc.vector.bn_aggr(mv[:, ct, :], stats[:, ct, :, :].rearrange("p q s -> p (q s)")
                                              ).then_inc(s_aggr, 1)
                        dve.wait_ge(s_aggr, 2 * (b + 1))
                        nc.vector.tensor_copy(mean[:, par, :], mv[:, :, 0]).then_inc(s_mean, 1)
                        nc.vector.tensor_scalar(vare[:, :], mv[:, :, 1], EPS, 2.0 ** (-2 * U_EXP),
                                                ALU.add, ALU.mult).then_inc(s_vare, 1)

                    def normalise(b, par, q):
                        if q == 0:
                            dve.wait_ge(s_rstd, b + 1)
                            dve.wait_ge(s_mean, b + 1)
                        for ct in range(CT):
                            n = 8 * b + 2 * q + ct
                            if not (isinstance(n, int) and n < 2):
                                dve.wait_ge(s_ul, n - 1)
                            nc.vector.tensor_scalar(u32[:, ct, :], xb[:, par, ct, q * CH:(q + 1) * CH],
                                                    mean[:, par, ct:ct + 1], rstd[:, par, ct:ct + 1],
                                                    ALU.subtract, ALU.mult).then_inc(s_u32, 1)

                    def ctx_absmax(b):
                        dve.wait_ge(s_ctx_in, 16 * (b + 1))
                        nc.vector.tensor_reduce(cmax[:, :], ctxr[:, :, :], AX.XY, ALU.max,
                                                apply_absolute_value=True).then_inc(s_cmax, 1)

                    def power_of_two(dst, rec, scale, src, exponent, sem_, base):
                        nc.vector.tensor_scalar(rec, src, TINY, None, ALU.max).then_inc(sem_, 1)
                        dve.wait_ge(sem_, base + 1)
                        nc.vector.tensor_scalar(dst.bitcast(U32), rec.bitcast(U32), EXPONENT, None,
                                                ALU.bitwise_and).then_inc(sem_, 1)
                        dve.wait_ge(sem_, base + 2)
                        nc.vector.reciprocal(rec, dst).then_inc(sem_, 1)
                        dve.wait_ge(sem_, base + 3)
                        nc.vector.tensor_scalar(scale, rec, 2.0 ** exponent, None, ALU.mult).then_inc(sem_, 1)

                    def ctx_scale(b, par):
                        dve.wait_ge(s_cmaxa, b + 1)
                        power_of_two(cpow[:, :], crec[:, :], cscale[:, :], cmaxa[:, :], IN_EXP, s_csc, 4 * b)
                        nc.vector.tensor_tensor(e_scale[:, par:par + 1], cpow[:, :], c_exp[:, :], ALU.mult
                                                ).then_inc(s_escale, 1)
                        nc.vector.tensor_tensor(a_att[:, par:par + 1], cpow[:, :], c_att[:, :], ALU.mult
                                                ).then_inc(s_escale, 1)

                    def ctx_low(b):
                        dve.wait_ge(s_ctxh, b + 1)
                        dve.wait_ge(s_csc, 4 * b + 4)
                        nc.vector.scalar_tensor_tensor(
                            out=ctxl[:, :, :].rearrange("p t m -> p (t m)"), in0=ctxr[:, :, :].rearrange("p t m -> p (t m)"),
                            scalar=cscale[:, 0:1], in1=ctxh[:, :, :].rearrange("p t m -> p (t m)"),
                            op0=ALU.mult, op1=ALU.subtract).then_inc(s_ctxl, 1)

                    def gv_low(b, par, which):
                        for k in range(2):
                            dve.wait_ge(s_gvh, 4 * b + 2 * which + k + 1)
                            dst, hi = (gl[:, par, k, :], gh[:, par, k, :]) if which == 0 else \
                                (vl[:, par, 2 * k:2 * k + 2, :].rearrange("p t c -> p (t c)"),
                                 vh[:, par, 2 * k:2 * k + 2, :].rearrange("p t c -> p (t c)"))
                            nc.vector.scalar_tensor_tensor(out=dst, in0=ps_p[which][k][:, :],
                                                           scalar=2.0 ** GV_EXP, in1=hi,
                                                           op0=ALU.mult, op1=ALU.subtract).then_inc(s_gv, 1)

                    def row_max(b, par, s):
                        j = TPB * b + s
                        dve.wait_ge(s_energy, j + 1)
                        nc.vector.tensor_reduce(nmax[:, s % 4:s % 4 + 1], ps_e[s % 2][:, :], AX.X, ALU.max,
                                                negate=True).then_inc(s_nmax, 1)
                        if s == 0:
                            dve.wait_ge(s_escale, 2 * (b + 1))
                        dve.wait_ge(s_nmax, j + 1)
                        nc.vector.tensor_tensor(nbias[:, s % 4:s % 4 + 1], nmax[:, s % 4:s % 4 + 1],
                                                e_scale[:, par:par + 1], ALU.mult).then_inc(s_nbias, 1)

                    def p_normalise(j, s):
                        dve.wait_ge(s_exp, j + 1)
                        nc.vector.reciprocal(rinv[:, s % 4:s % 4 + 1], rsum[:, s % 4:s % 4 + 1]).then_inc(s_rinv, 1)
                        dve.wait_ge(s_rinv, j + 1)
                        nc.vector.tensor_scalar(pf[:, s % 4, :], pf[:, s % 4, :], rinv[:, s % 4:s % 4 + 1],
                                                2.0 ** P_EXP, ALU.mult, ALU.mult).then_inc(s_pn, 1)

                    def p_low(j, s):
                        dve.wait_ge(s_pth, j + 1)
                        cols = slice((s % TPC) * P, (s % TPC + 1) * P)
                        nc.vector.tensor_tensor(ptl[:, (s // TPC) % 2, :, cols],
                                                ps_t[s % 2][:, :].rearrange("p (t n) -> p t n", t=MT),
                                                pth[:, (s // TPC) % 2, :, cols], ALU.subtract).then_inc(s_ptl, 1)

                    def gather_x1(pair):
                        b, par, q, ct, n, bank = pair
                        x1 = xb[:, par, ct, q * CH:(q + 1) * CH]
                        done = 2 * NQ * b + 2 * q + ct
                        dve.wait_ge(s_pair, n + 1)
                        nc.vector.scalar_tensor_tensor(out=x1, in0=ps_p[bank][0][:, :], scalar=a_skip[:, 0:1],
                                                       in1=x1, op0=ALU.mult, op1=ALU.add).then_inc(s_skip_add, 1)
                        dve.wait_ge(s_skip_add, done + 1)
                        nc.vector.scalar_tensor_tensor(out=x1, in0=ps_p[bank][1][:, :], scalar=a_att[:, par:par + 1],
                                                       in1=x1, op0=ALU.mult, op1=ALU.add).then_inc(s_x1, 1)

                    dve.wait_ge(s_half, 1)
                    ctx_absmax(0)
                    stats_of(0, 0, range(8))
                    aggregate(0, 0)
                    for i in range(3):
                        dve.wait_ge(s_wt_ps, i + 1)
                        for k in range(CT):
                            nc.vector.tensor_copy(wt32[:, i, k, :], ps_p[i % 2][k][:, 0:C]).then_inc(s_wt32, 1)
                        dve.wait_ge(s_wt32, 2 * i + 2)
                        nc.vector.tensor_reduce(wmax[:, i:i + 1], wt32[:, i, :, :], AX.XY, ALU.max,
                                                apply_absolute_value=True).then_inc(s_wmax, 1)
                    dve.wait_ge(s_wmaxa, 1)
                    power_of_two(wpow[:, :], wrec[:, :], wscale[:, :], wmaxa[:, :], IN_EXP, s_wsc, 0)
                    dve.wait_ge(s_wsc, 4)
                    nc.vector.tensor_scalar(c_exp[:, :], wpow[:, 0:1], 2.0 ** (-4 - U_EXP - GV_EXP - 2 * IN_EXP),
                                            None, ALU.mult).then_inc(s_wsc, 1)
                    dve.wait_ge(s_tanh, 1)
                    nc.vector.tensor_scalar(c_att[:, :], wpow[:, 1:2], tg[:, 0:1],
                                            2.0 ** (-P_EXP - GV_EXP - 2 * IN_EXP), ALU.mult, ALU.mult
                                            ).then_inc(s_wsc, 1)
                    nc.vector.tensor_scalar(a_skip[:, :], wpow[:, 2:3], tg[:, 0:1],
                                            2.0 ** (-U_EXP - IN_EXP), ALU.mult, ALU.mult).then_inc(s_wsc, 1)
                    dve.wait_ge(s_wsc, 7)
                    ctx_scale(0, 0)
                    ctx_low(0)
                    for i in range(3):
                        dve.wait_ge(s_wth, i + 1)
                        nc.vector.scalar_tensor_tensor(
                            out=wtl[:, i, :, :].rearrange("p t c -> p (t c)"),
                            in0=wt32[:, i, :, :].rearrange("p t c -> p (t c)"), scalar=wscale[:, i:i + 1],
                            in1=wth[:, i, :, :].rearrange("p t c -> p (t c)"),
                            op0=ALU.mult, op1=ALU.subtract).then_inc(s_wtl, 1)
                    normalise(0, 0, 0)
                    gv_low(0, 0, 0)
                    gv_low(0, 0, 1)
                    normalise(0, 0, 1)
                    dve.wait_ge(s_bias_in, 16)
                    nc.vector.tensor_scalar(biasg[:, :], biasg[:, :], tg[:, 1:2], None, ALU.mult).then_inc(s_biasg, 1)

                    def emit(b, par, first, last):
                        for s in range(TPB):
                            j = TPB * b + s
                            row_max(b, par, s)
                            if not (first and s < 1):
                                p_normalise(j - 1, (s - 1) % TPB)
                            if not (first and s < 3):
                                p_low(j - 3, (s - 3) % TPB)
                            if s == 0 and not first:
                                gather_x1(attention_pair(b - 1, 1 - par, TPB - 1, False, False))
                            elif s > 0 and attention_pair(b, par, s - 1, first, last):
                                gather_x1(attention_pair(b, par, s - 1, first, last))
                            if s == 2:
                                normalise(b, par, 2)
                            if s == 6:
                                normalise(b, par, 3)
                            if not last:
                                if s == 3:
                                    ctx_absmax(b + 1)
                                if s == 6:
                                    ctx_scale(b + 1, 1 - par)
                                if s == 7:
                                    ctx_low(b + 1)
                                if s - 1 in GV:
                                    gv_low(b + 1, 1 - par, GV[s - 1][0])
                                if s in (8, 9, 10, 11):
                                    stats_of(b + 1, 1 - par, range(2 * (s - 8), 2 * (s - 8) + 2))
                                if s == 12:
                                    aggregate(b + 1, 1 - par)
                                if s == 13:
                                    normalise(b + 1, 1 - par, 0)
                                if s == 15:
                                    normalise(b + 1, 1 - par, 1)

                    batches(emit, dve)
                    p_normalise(TPB * B - 1, TPB - 1)
                    for s in (TPB - 3, TPB - 2, TPB - 1):
                        p_low(TPB * (B - 1) + s, s)
                    gather_x1(attention_pair(B - 1, (B - 1) % 2, TPB - 1, False, True))
                    for s in OLD:
                        gather_x1(tail_pair(s))

                @block.tensor
                def _(pe):
                    def split_product(dst, terms, finish):
                        ops = [(lo_l if k == 2 else hi_l, lo_r if k == 1 else hi_r)
                               for (hi_l, lo_l), (hi_r, lo_r) in terms for k in range(3)]
                        for n, (lhs, rhs) in enumerate(ops):
                            ins = nc.tensor.matmul(dst, lhs, rhs, start=n == 0, stop=n == len(ops) - 1)
                        if finish is not None:
                            ins.then_inc(finish, 1)

                    pe.wait_ge(s_w_in, 64)
                    for k in range(CT):
                        for o in range(CT):
                            ins = nc.tensor.matmul(ps_p[0][k][:, 0:C], w_nat[:, 1, o, k * P:(k + 1) * P],
                                                   w_nat[:, 0, o, :], start=o == 0, stop=o == CT - 1)
                    ins.then_inc(s_wt_ps, 1)
                    pe.wait_ge(s_ident, 1)
                    for i in (1, 2):
                        if i == 2:
                            pe.wait_ge(s_wt32, 2)
                        for k in range(CT):
                            for o in range(CT):
                                ins = nc.tensor.transpose(ps_p[i % 2][k][:, o * P:(o + 1) * P],
                                                          w_nat[:, i + 1, o, k * P:(k + 1) * P], ident[:, :])
                        ins.then_inc(s_wt_ps, 1)

                    def g_or_v(b, par, which, bank):
                        if which == 0:
                            pe.wait_ge(s_ctxl, b + 1)
                            for ct in range(CT):
                                split_product(ps_p[bank][ct][:, :],
                                              [((wth[:, 0, k, ct * P:(ct + 1) * P], wtl[:, 0, k, ct * P:(ct + 1) * P]),
                                                (ctxh[:, k, :], ctxl[:, k, :])) for k in range(CT)],
                                              s_pair if ct == CT - 1 else None)
                        else:
                            for mt in range(MT):
                                split_product(ps_p[bank][mt // 2][:, (mt % 2) * C:(mt % 2 + 1) * C],
                                              [((ctxh[:, k, mt * P:(mt + 1) * P], ctxl[:, k, mt * P:(mt + 1) * P]),
                                                (wth[:, 1, k, :], wtl[:, 1, k, :])) for k in range(CT)],
                                              s_pair if mt == MT - 1 else None)

                    pe.wait_ge(s_wtl, 3)
                    g_or_v(0, 0, 0, 0)
                    g_or_v(0, 0, 1, 1)

                    def energy(b, par, s, first):
                        j = TPB * b + s
                        if s % TPC == 0:
                            pe.wait_ge(s_ul, 8 * b + 2 * (s // TPC) + 2)
                        if s == 0:
                            pe.wait_ge(s_gv, 4 * b + 2)
                        if not (first and s < 2):
                            pe.wait_ge(s_exp, j - 1)
                        split_product(ps_e[s % 2][:, :],
                                      [((uh[:, k, s * P:(s + 1) * P], ul[:, k, s * P:(s + 1) * P]),
                                        (gh[:, par, k, :], gl[:, par, k, :])) for k in range(CT)], s_energy)

                    def transpose_p(j, s):
                        pe.wait_ge(s_pn, j + 1)
                        if not (isinstance(j, int) and j < 2):
                            pe.wait_ge(s_ptl, j - 1)
                        for mt in range(MT):
                            ins = nc.tensor.transpose(ps_t[s % 2][:, mt * P:(mt + 1) * P],
                                                      pf[:, s % 4, mt * P:(mt + 1) * P], ident[:, :])
                        ins.then_inc(s_t, 1)

                    def attend(pair, free):
                        b, par, q, ct, n, bank = pair
                        cols = slice(q * CH, (q + 1) * CH)
                        rows = slice(ct * P, (ct + 1) * P)
                        pe.wait_ge(*free)
                        split_product(ps_p[bank][0][:, :],
                                      [((wth[:, 2, k, rows], wtl[:, 2, k, rows]), (uh[:, k, cols], ul[:, k, cols]))
                                       for k in range(CT)], None)
                        if ct == 0:
                            pe.wait_ge(s_ptl, TPB * b + TPC * (q + 1))
                            if q == 0:
                                pe.wait_ge(s_gv, 4 * b + 4)
                        split_product(ps_p[bank][1][:, :],
                                      [((vh[:, par, m, rows], vl[:, par, m, rows]),
                                        (pth[:, q % 2, m, :], ptl[:, q % 2, m, :])) for m in range(MT)], s_pair)

                    def pair_read(b, s, first, last):
                        if first and s in (7, 8):
                            return s_gv, 2 * (s - 6)
                        if s in (11, 12) and not last:
                            return s_gv, 4 * (b + 1) + 2 * (s - 10)
                        ahead = {0: -4, 3: -3, 4: -2, 7: -1, 8: 0, 9: 1, 10: 2, 11: 1, 12: 2, 15: 3}
                        return s_x1, 2 * NQ * b + ahead[s]

                    def emit(b, par, first, last):
                        for s in range(TPB):
                            energy(b, par, s, first)
                            if not (first and s < 2):
                                transpose_p(TPB * b + s - 2, (s - 2) % TPB)
                            pair = attention_pair(b, par, s, first, last)
                            if pair:
                                attend(pair, pair_read(b, s, first, last))
                            if not last and s in GV:
                                pe.wait_ge(*pair_read(b, s, first, last))
                                g_or_v(b + 1, 1 - par, GV[s][0], BANK[s])

                    batches(emit, pe)
                    for s in (TPB - 2, TPB - 1):
                        transpose_p(TPB * (B - 1) + s, s)
                    for s in OLD:
                        attend(tail_pair(s), pair_read(B, s, False, False))

        with ExitStack() as phase:
            def sb(name, shape, dt):
                return phase.enter_context(nc.sbuf_tensor(name, shape, dt))

            def ps(name):
                return phase.enter_context(nc.psum_tensor(name, [P, CH], F32))

            wh = sb("wh", [P, OC * KT, CH], F16)
            wl = sb("wl", [P, OC * KT, CH], F16)
            u2h = sb("u2h", [P, 2, KT, P], F16)
            u2l = sb("u2l", [P, 2, KT, P], F16)
            fmax = sb("fmax", [P, 3], F32)
            fmaxa = sb("fmaxa", [P, 3], F32)
            fbound = sb("fbound", [P, 2], F32)
            fpow = sb("fpow", [P, 1], F32)
            frec = sb("frec", [P, 1], F32)
            fscale = sb("fscale", [P, 1], F32)
            a_ffn = sb("a_ffn", [P, 1], F32)
            stats2 = sb("stats2", [P, 4, 6], F32)
            mv2 = sb("mv2", [P, 2], F32)
            vare2 = sb("vare2", [P, 1], F32)
            rstd2 = sb("rstd2", [P, 1], F32)

            ps_w = [ps(f"ps_w{i}") for i in range(4)]
            ps_u = [ps("ps_u0"), ps("ps_u1")]
            ps_f = [ps("ps_f0"), ps("ps_f1")]

            s_bt_ps = sem("s_bt_ps")
            s_bt = sem("s_bt")
            s_fmax = sem("s_fmax")
            s_fmaxa = sem("s_fmaxa")
            s_fsc = sem("s_fsc")
            s_unit = sem("s_unit")
            s_wh = sem("s_wh")
            s_wl = sem("s_wl")
            s_row_in = [sem(f"s_row_in{i}") for i in range(4)]
            s_out_stored = sem("s_out_stored")
            s_stats2 = sem("s_stats2")
            s_aggr2 = sem("s_aggr2")
            s_vare2 = sem("s_vare2")
            s_rstd2 = sem("s_rstd2")
            s_u2 = sem("s_u2")
            s_xbias = sem("s_xbias")
            s_ut = sem("s_ut")
            s_u2h = sem("s_u2h")
            s_u2l = sem("s_u2l")
            s_f = sem("s_f")
            s_out = sem("s_out")

            def row_tiles(emit, eng):
                for r in range(4):
                    emit(r, 0, r, r == 0, False)
                with eng.Fori(1, ST // 4 - 1) as i:
                    for r in range(4):
                        emit(4 * i + r, i, r, False, False)
                for r in range(4):
                    emit(ST - 4 + r, ST // 4 - 1, r, False, r == 3)

            with nc.Block() as block:

                @block.sync
                def _(sp):
                    def load_row(i, r):
                        sp.dma_start(xring[:, r, :], x1_tiles[i, :, :]).then_inc(s_row_in[r], 16)

                    load_row(0, 0)
                    for blk in range(2, 16):
                        sp.wait_ge(s_unit, 4 * (blk - 1))
                        load_w_block(sp, blk)
                    sp.wait_ge(s_unit, OC * KT)
                    load_row(1, 1)
                    load_row(2, 2)

                    def emit(i, f, r, first, last):
                        if not (isinstance(i, int) and i + 3 >= ST):
                            if not first:
                                sp.wait_ge(s_out_stored, 16 * i)
                            load_row(i + 3, (r + 3) % 4)
                        if last:
                            for oc in range(OC):
                                sp.wait_ge(s_out, OC * i + oc + 1)
                                sp.dma_start(out_tiles[i, :, oc * CH:(oc + 1) * CH],
                                             xring[:, r, oc * CH:(oc + 1) * CH]).then_inc(s_out_stored, 16)
                        else:
                            sp.wait_ge(s_out, OC * (i + 1))
                            sp.dma_start(out_tiles[i, :, :], xring[:, r, :]).then_inc(s_out_stored, 16)

                    row_tiles(emit, sp)
                    sp.wait_ge(s_out_stored, 16 * (ST - 1 + OC))

                @block.gpsimd
                def _(pool):
                    pool.wait_ge(s_fmax, 3)
                    nc.gpsimd.partition_all_reduce(fmaxa[:, :], fmax[:, :], P, RMAX).then_inc(s_fmaxa, 1)

                    def prepare(i, r):
                        pool.wait_ge(s_vare2, i + 1)
                        nc.gpsimd.tensor_tensor(rstd2[:, :], vare2[:, :], minus_half[:, 0:1],
                                                ALU.pow).then_inc(s_rstd2, 1)
                        pool.wait_ge(s_u2, i + 1)
                        nc.gpsimd.tensor_tensor(xring[:, r, :], xring[:, r, :], biasg[:, :],
                                                ALU.add).then_inc(s_xbias, 1)

                    def emit(i, f, r, first, last):
                        if not last:
                            prepare(i + 1, (r + 1) % 4)

                    prepare(0, 0)
                    row_tiles(emit, pool)

                @block.scalar
                def _(act):
                    act.wait_ge(s_fsc, 7)

                    with act.Fori(0, OC) as oc:
                        for kt in range(KT):
                            act.wait_ge(s_unit, KT * oc + kt + 1)
                            nc.scalar.activation(wh[:, bass.ds(KT * oc + kt, 1), :], ps_w[kt % 4][:, None, :],
                                                 ACT.Copy, scale=fscale[:, 0:1]).then_inc(s_wh, 1)

                    def u2_high(i, r):
                        for k in range(4):
                            act.wait_ge(s_ut, 4 * i + k + 1)
                            nc.scalar.activation(u2h[:, r % 2, 4 * k:4 * k + 4, :].rearrange("p t n -> p (t n)"),
                                                 ps_u[k % 2][:, :], ACT.Copy).then_inc(s_u2h, 1)

                    def emit(i, f, r, first, last):
                        if not last:
                            u2_high(i + 1, r + 1)

                    u2_high(0, 0)
                    row_tiles(emit, act)

                @block.vector
                def _(dve):
                    dve.wait_ge(s_lora_in, 16 * (1 + 2 * NADAPT))
                    for g in range(4):
                        dve.wait_ge(s_bt_ps, g + 1)
                        nc.vector.tensor_scalar(
                            bt[:, :].rearrange("q (p t) -> q t p", t=KT)[:, 4 * g:4 * g + 4, :],
                            ps_w[g][:, :].rearrange("q (t p) -> q t p", t=4), coef[:, 0:1], LORA_SCALE,
                            ALU.mult, ALU.mult).then_inc(s_bt, 1)
                    nc.vector.tensor_reduce(fmax[:, 0:1], a_nat, AX.X, ALU.max,
                                            apply_absolute_value=True).then_inc(s_fmax, 1)
                    nc.vector.tensor_reduce(fmax[:, 2:3], wabs[:, :], AX.X, ALU.max).then_inc(s_fmax, 1)
                    dve.wait_ge(s_bt, 4)
                    nc.vector.tensor_reduce(fmax[:, 1:2], bt[:, :], AX.X, ALU.max,
                                            apply_absolute_value=True).then_inc(s_fmax, 1)
                    dve.wait_ge(s_fmaxa, 1)
                    nc.vector.tensor_tensor(fbound[:, 0:1], fmaxa[:, 0:1], fmaxa[:, 1:2], ALU.mult).then_inc(s_fsc, 1)
                    dve.wait_ge(s_fsc, 1)
                    nc.vector.scalar_tensor_tensor(out=fbound[:, 1:2], in0=fbound[:, 0:1], scalar=float(P),
                                                   in1=fmaxa[:, 2:3], op0=ALU.mult, op1=ALU.add).then_inc(s_fsc, 1)
                    dve.wait_ge(s_fsc, 2)
                    nc.vector.tensor_scalar(frec[:, :], fbound[:, 1:2], TINY, None, ALU.max).then_inc(s_fsc, 1)
                    dve.wait_ge(s_fsc, 3)
                    nc.vector.tensor_scalar(fpow[:, :].bitcast(U32), frec[:, :].bitcast(U32), EXPONENT, None,
                                            ALU.bitwise_and).then_inc(s_fsc, 1)
                    dve.wait_ge(s_fsc, 4)
                    nc.vector.reciprocal(frec[:, :], fpow[:, :]).then_inc(s_fsc, 1)
                    nc.vector.tensor_scalar(a_ffn[:, :], fpow[:, :], tg[:, 1:2], 2.0 ** (-U_EXP - W_EXP),
                                            ALU.mult, ALU.mult).then_inc(s_fsc, 1)
                    dve.wait_ge(s_fsc, 6)
                    nc.vector.tensor_scalar(fscale[:, :], frec[:, :], 2.0 ** W_EXP, None, ALU.mult).then_inc(s_fsc, 1)
                    dve.wait_ge(s_fsc, 7)

                    def prepare(i, f, r):
                        dve.wait_ge(s_row_in[r], 16 * (f + 1))
                        for q in range(4):
                            nc.vector.bn_stats(stats2[:, q, :], xring[:, r, q * CH:(q + 1) * CH]).then_inc(s_stats2, 1)
                        dve.wait_ge(s_stats2, 4 * (i + 1))
                        nc.vector.tensor_copy(idle_dve[:, :], minus_half[:, 0:1])
                        nc.vector.bn_aggr(mv2[:, :], stats2[:, :, :].rearrange("p q s -> p (q s)")).then_inc(s_aggr2, 1)
                        dve.wait_ge(s_aggr2, i + 1)
                        nc.vector.tensor_scalar(vare2[:, :], mv2[:, 1:2], EPS, 2.0 ** (-2 * U_EXP),
                                                ALU.add, ALU.mult).then_inc(s_vare2, 1)
                        dve.wait_ge(s_rstd2, i + 1)
                        if not (isinstance(i, int) and i == 0):
                            dve.wait_ge(s_ut, 4 * i)
                        nc.vector.tensor_scalar(u2[:, :], xring[:, r, :], mv2[:, 0:1], rstd2[:, 0:1],
                                                ALU.subtract, ALU.mult).then_inc(s_u2, 1)

                    def u2_low(i, r, ks):
                        for k in ks:
                            dve.wait_ge(s_u2h, 4 * i + k + 1)
                            nc.vector.tensor_tensor(u2l[:, r % 2, 4 * k:4 * k + 4, :].rearrange("p t n -> p (t n)"),
                                                    ps_u[k % 2][:, :],
                                                    u2h[:, r % 2, 4 * k:4 * k + 4, :].rearrange("p t n -> p (t n)"),
                                                    ALU.subtract).then_inc(s_u2l, 1)

                    def finish(i, r, oc):
                        dve.wait_ge(s_f, OC * i + oc + 1)
                        if oc == 0:
                            dve.wait_ge(s_xbias, i + 1)
                        o = xring[:, r, oc * CH:(oc + 1) * CH]
                        nc.vector.scalar_tensor_tensor(out=o, in0=ps_f[oc % 2][:, :], scalar=a_ffn[:, 0:1], in1=o,
                                                       op0=ALU.mult, op1=ALU.add).then_inc(s_out, 1)

                    prepare(0, 0, 0)
                    with dve.Fori(0, OC) as oc:
                        for kt in range(KT):
                            dve.wait_ge(s_wh, KT * oc + kt + 1)
                            n = bass.ds(KT * oc + kt, 1)
                            nc.vector.scalar_tensor_tensor(
                                out=wl[:, n, :], in0=ps_w[kt % 4][:, None, :], scalar=fscale[:, 0:1],
                                in1=wh[:, n, :], op0=ALU.mult, op1=ALU.subtract).then_inc(s_wl, 1)
                    u2_low(0, 0, range(4))

                    def emit(i, f, r, first, last):
                        if not last:
                            prepare(i + 1, f + (1 if r == 3 else 0), (r + 1) % 4)
                        finish(i, r, 0)
                        if not last:
                            u2_low(i + 1, r + 1, (0, 1))
                        finish(i, r, 1)
                        if not last:
                            u2_low(i + 1, r + 1, (2, 3))
                        finish(i, r, 2)
                        finish(i, r, 3)

                    row_tiles(emit, dve)

                @block.tensor
                def _(pe):
                    pe.wait_ge(s_lora_in, 16 * (1 + 2 * NADAPT))
                    for g in range(4):
                        for t in range(4):
                            ins = nc.tensor.transpose(ps_w[g][:, t * P:(t + 1) * P], b_nat[:, 4 * g + t, :, :].rearrange("p n r -> p (n r)"),
                                                      ident[:, :])
                        ins.then_inc(s_bt_ps, 1)
                    pe.wait_ge(s_bt, 4)

                    def unit(oc, kt):
                        if kt % 4 == 0:
                            pe.wait_ge(s_wstage[(kt // 4) % 2], 32 * oc + 16 * (kt // 8 + 1))
                        if not (isinstance(oc, int) and kt < 4):
                            pe.wait_ge(s_wl, KT * oc + kt - 3)
                        for t in range(4):
                            nc.tensor.matmul(ps_w[kt % 4][:, t * P:(t + 1) * P],
                                             w_stage[(kt // 4) % 2][:, t, (kt % 4) * P:(kt % 4 + 1) * P],
                                             ident[:, :], is_transpose=True, start=t == 0, stop=False)
                        nc.tensor.matmul(ps_w[kt % 4][:, :], a_nat[:, kt * P:(kt + 1) * P],
                                         bt[:, bass.ds(CH * oc, CH)], start=False, stop=True).then_inc(s_unit, 1)

                    for kt in range(KT):
                        unit(0, kt)
                    with pe.Fori(1, OC) as oc:
                        for kt in range(KT):
                            unit(oc, kt)

                    def transpose_rows(i, r, k):
                        n = 4 * i + k
                        if k == 0:
                            pe.wait_ge(s_u2, i + 1)
                        if not (isinstance(n, int) and n < 2):
                            pe.wait_ge(s_u2l, n - 1)
                        for t in range(4):
                            ins = nc.tensor.transpose(ps_u[k % 2][:, t * P:(t + 1) * P],
                                                      u2[:, (4 * k + t) * P:(4 * k + t + 1) * P], ident[:, :])
                        ins.then_inc(s_ut, 1)

                    def product(i, r, oc):
                        if oc == 0:
                            pe.wait_ge(s_u2l, 4 * (i + 1))
                        if isinstance(i, int) and i == 0:
                            pe.wait_ge(s_wl, KT * (oc + 1))
                        if not (isinstance(i, int) and i == 0 and oc < 2):
                            pe.wait_ge(s_out, OC * i + oc - 1)
                        for kt in range(KT):
                            hi, lo = u2h[:, r % 2, kt, :], u2l[:, r % 2, kt, :]
                            n = oc * KT + kt
                            nc.tensor.matmul(ps_f[oc % 2][:, :], hi, wh[:, n, :], start=kt == 0, stop=False)
                            nc.tensor.matmul(ps_f[oc % 2][:, :], hi, wl[:, n, :], start=False, stop=False)
                            ins = nc.tensor.matmul(ps_f[oc % 2][:, :], lo, wh[:, n, :], start=False,
                                                   stop=kt == KT - 1)
                        ins.then_inc(s_f, 1)

                    for k in range(4):
                        transpose_rows(0, 0, k)

                    def emit(i, f, r, first, last):
                        product(i, r, 0)
                        if not last:
                            transpose_rows(i + 1, r + 1, 0)
                            transpose_rows(i + 1, r + 1, 1)
                        product(i, r, 1)
                        if not last:
                            transpose_rows(i + 1, r + 1, 2)
                            transpose_rows(i + 1, r + 1, 3)
                        product(i, r, 2)
                        product(i, r, 3)

                    row_tiles(emit, pe)


_INS = ["x", "ctx_1024", "g_xattn", "g_ffn", "L0_xattn_Wq", "L0_xattn_Wk", "L0_xattn_Wv", "L0_xattn_Wskip",
        "L0_ffn_lora_A", "L0_ffn_lora_B", "L0_ffn_W", "L0_ffn_bias", "L0_ffn_lora_weights"]


def kernel(**inputs):
    import numpy as _np
    import concourse.bacc as _bacc
    from concourse import mybir as _mybir
    from concourse.bass_utils import run_bass_kernel_spmd as _run

    nc = _bacc.Bacc("TRN2", target_bir_lowering=False, num_devices=1)
    arrays, args = {}, []
    for name in _INS:
        a = _np.ascontiguousarray(inputs[name])
        arrays[f"in_{name}"] = a
        args.append(nc.dram_tensor(f"in_{name}", a.shape, _mybir.dt.from_np(a.dtype), kind="ExternalInput").ap())
    args.append(nc.dram_tensor("out_0", inputs["x"].shape, _mybir.dt.float32, kind="ExternalOutput").ap())
    flamingo_kernel(nc, *args)
    r = _run(nc, [arrays], core_ids=[0])
    return r.results[0]["out_0"]
```

```python
from contextlib import ExitStack

import concourse.bass as bass
from concourse import mybir

F32 = mybir.dt.float32
F16 = mybir.dt.float16
U32 = mybir.dt.uint32
ALU = mybir.AluOpType
ACT = mybir.ActivationFunctionType
AX = mybir.AxisListType
RMAX = bass.bass_isa.ReduceOp.max

P = 128
EXPONENT = 0x7F800000
TINY = 1e-30
EPS = 1e-5
U_EXP = 10
P_EXP = 14
IN_EXP = 6
GV_EXP = -7
W_EXP = 14
LORA_SCALE = 2.0


def flamingo_kernel(nc, x, ctx_in, g_xattn, g_ffn, wq, wk, wv, wskip, lora_a, lora_b, w, bias,
                    lora_weights, out):
    B, C, N = x.shape
    M = ctx_in.shape[2]
    NADAPT, RANK, D = lora_a.shape
    O = w.shape[0]
    CT = C // P
    MT = M // P
    CH = 512
    NQ = N // CH
    TPC = CH // P
    TPB = N // P
    KT = D // P
    OC = O // CH
    ST = B * C // P
    XPB = CT * NQ
    assert CT == 2 and MT == 4 and NQ == 4 and TPC == 4 and NADAPT * RANK == P

    x1_dram = nc.dram_tensor("x1_scratch", [B, C, N], F32, kind="Internal").ap()
    x_rows = x.rearrange("b (t p) n -> b p t n", p=P)
    x1_rows = x1_dram.rearrange("b (t p) n -> b p t n", p=P)
    x1_tiles = x1_dram.rearrange("b (t p) n -> (b t) p n", p=P)
    out_tiles = out.rearrange("b (t p) n -> (b t) p n", p=P)
    ctx_rows = ctx_in.rearrange("b (t p) m -> b p t m", p=P)

    with ExitStack() as outer:
        def sem(name):
            return outer.enter_context(nc.semaphore(name))

        def keep(name, shape, dt):
            return outer.enter_context(nc.sbuf_tensor(name, shape, dt))

        ident = keep("ident", [P, P], F32)
        xring = keep("xring", [P, 4, D], F32)
        u2 = keep("u2", [P, D], F32)
        bt = keep("bt", [P, O], F32)
        biasg = keep("biasg", [P, O], F32)
        tg = keep("tg", [P, 2], F32)
        coef = keep("coef", [P, 1], F32)
        wabs = keep("wabs", [P, O * D // (P * 1024)], F32)
        minus_half = keep("minus_half", [P, 2], F32)
        idle_pool = keep("idle_pool", [P, 1], F32)
        idle_dve = keep("idle_dve", [P, 1], F32)
        a_nat = xring[:, 1, :]
        w_stage = [xring[:, 2 + i, :].rearrange("p (t d) -> p t d", t=4) for i in range(2)]
        b_nat = u2[:, :].rearrange("p (t n r) -> p t n r", n=NADAPT, r=RANK)

        s_ident0 = sem("s_ident0")
        s_ident = sem("s_ident")
        s_lora_in = sem("s_lora_in")
        s_wstage = [sem("s_wstage0"), sem("s_wstage1")]

        def load_w_block(eng, blk):
            oc, db = blk // 4, blk % 4
            src = w[oc * CH:(oc + 1) * CH, db * 512:(db + 1) * 512].rearrange("(t p) d -> p t d", p=P)
            eng.dma_start(w_stage[blk % 2], src).then_inc(s_wstage[blk % 2], 16)

        with ExitStack() as phase:
            def sb(name, shape, dt):
                return phase.enter_context(nc.sbuf_tensor(name, shape, dt))

            def ps(name):
                return phase.enter_context(nc.psum_tensor(name, [P, CH], F32))

            xb = sb("xb", [P, 2, CT, N], F32)
            uh = sb("uh", [P, CT, N], F16)
            ul = sb("ul", [P, CT, N], F16)
            u32 = sb("u32", [P, CT, CH], F32)
            pf = sb("pf", [P, 4, M], F32)
            pth = sb("pth", [P, 2, MT, CH], F16)
            ptl = sb("ptl", [P, 2, MT, CH], F16)
            ctxr = sb("ctxr", [P, CT, M], F32)
            ctxh = sb("ctxh", [P, CT, M], F16)
            ctxl = sb("ctxl", [P, CT, M], F16)
            gh = sb("gh", [P, 2, CT, M], F16)
            gl = sb("gl", [P, 2, CT, M], F16)
            vh = sb("vh", [P, 2, MT, C], F16)
            vl = sb("vl", [P, 2, MT, C], F16)
            w_nat = sb("w_nat", [P, 4, CT, C], F32)
            wt32 = sb("wt32", [P, 3, CT, C], F32)
            wth = sb("wth", [P, 3, CT, C], F16)
            wtl = sb("wtl", [P, 3, CT, C], F16)
            wscan = sb("wscan", [P, 2, 1024], F32)
            wjunk = sb("wjunk", [P, 1024], F32)
            gates = sb("gates", [P, 2], F32)
            wmax = sb("wmax", [P, 3], F32)
            wmaxa = sb("wmaxa", [P, 3], F32)
            wpow = sb("wpow", [P, 3], F32)
            wrec = sb("wrec", [P, 3], F32)
            wscale = sb("wscale", [P, 3], F32)
            c_exp = sb("c_exp", [P, 1], F32)
            c_att = sb("c_att", [P, 1], F32)
            a_skip = sb("a_skip", [P, 1], F32)
            cmax = sb("cmax", [P, 1], F32)
            cmaxa = sb("cmaxa", [P, 1], F32)
            cpow = sb("cpow", [P, 1], F32)
            crec = sb("crec", [P, 1], F32)
            cscale = sb("cscale", [P, 1], F32)
            e_scale = sb("e_scale", [P, 2], F32)
            a_att = sb("a_att", [P, 2], F32)
            nmax = sb("nmax", [P, 4], F32)
            nbias = sb("nbias", [P, 4], F32)
            rsum = sb("rsum", [P, 4], F32)
            rinv = sb("rinv", [P, 4], F32)
            stats = sb("stats", [P, CT, NQ, 6], F32)
            mv = sb("mv", [P, CT, 2], F32)
            vare = sb("vare", [P, CT], F32)
            rstd = sb("rstd", [P, 2, CT], F32)
            mean = sb("mean", [P, 2, CT], F32)

            ps_e = [ps("ps_e0"), ps("ps_e1")]
            ps_t = [ps("ps_t0"), ps("ps_t1")]
            ps_s = [ps("ps_s0"), ps("ps_s1")]
            ps_a = [ps("ps_a0"), ps("ps_a1")]
            ps_gv = [ps_s[0], ps_a[0], ps_s[1], ps_a[1]]

            s_w_in = sem("s_w_in")
            s_gates_in = sem("s_gates_in")
            s_tanh = sem("s_tanh")
            s_half = sem("s_half")
            s_biasg = sem("s_biasg")
            s_bias_in = sem("s_bias_in")
            s_wt_ps = sem("s_wt_ps")
            s_wt32 = sem("s_wt32")
            s_wmax = sem("s_wmax")
            s_wmaxa = sem("s_wmaxa")
            s_wsc = sem("s_wsc")
            s_wth = sem("s_wth")
            s_wtl = sem("s_wtl")
            s_x_in = [[sem(f"s_x_in{i}{q}") for q in range(NQ)] for i in range(2)]
            s_ctx_in = sem("s_ctx_in")
            s_x1_stored = [sem(f"s_x1_stored{q}") for q in range(NQ)]
            s_scan_in = [sem("s_scan_in0"), sem("s_scan_in1")]
            s_scanned = sem("s_scanned")
            s_stats = sem("s_stats")
            s_aggr = sem("s_aggr")
            s_vare = sem("s_vare")
            s_rstd = sem("s_rstd")
            s_u32 = sem("s_u32")
            s_uh = sem("s_uh")
            s_ul = sem("s_ul")
            s_cmax = sem("s_cmax")
            s_cmaxa = sem("s_cmaxa")
            s_csc = sem("s_csc")
            s_ctxh = sem("s_ctxh")
            s_ctxl = sem("s_ctxl")
            s_gvh = sem("s_gvh")
            s_gv = sem("s_gv")
            s_energy = sem("s_energy")
            s_nmax = sem("s_nmax")
            s_nbias = sem("s_nbias")
            s_exp = sem("s_exp")
            s_rinv = sem("s_rinv")
            s_pn = sem("s_pn")
            s_t = sem("s_t")
            s_pth = sem("s_pth")
            s_ptl = sem("s_ptl")
            s_skip = sem("s_skip")
            s_att = sem("s_att")
            s_gv_ps = sem("s_gv_ps")
            s_a_att = sem("s_a_att")
            s_escale = sem("s_escale")
            s_mean = sem("s_mean")
            s_skip_add = sem("s_skip_add")
            s_x1 = sem("s_x1")

            SCANS = O * D // (P * 1024)
            SPB = SCANS // B
            assert SPB == 2
            w_pieces = w.rearrange("o (h d) -> (o h) d", d=1024).rearrange("(n p) d -> n p d", p=P)

            LAG = 7

            def piece(b, par, s, first):
                if first and s < LAG:
                    return None
                q, rest = divmod(s - LAG if s >= LAG else s - LAG + TPB, 2 * CT)
                return (b, par, q, rest // 2, rest % 2) if s >= LAG else (b - 1, 1 - par, q, rest // 2, rest % 2)

            GV = {9: 0, 10: 1, 11: 2, 12: 3}

            def batches(emit, eng):
                emit(0, 0, True, False)
                with eng.Fori(0, (B - 2) // 2) as i:
                    emit(2 * i + 1, 1, False, False)
                    emit(2 * i + 2, 0, False, False)
                emit(B - 1, (B - 1) % 2, False, True)

            with nc.Block() as block:

                @block.sync
                def _(sp):
                    def store_x1(b, par, q, ct, n):
                        sp.wait_ge(s_x1, n + 1)
                        sp.dma_start(x1_rows[b, :, ct, q * CH:(q + 1) * CH],
                                     xb[:, par, ct, q * CH:(q + 1) * CH]).then_inc(s_x1_stored[q], 16)

                    def load_x(b, par, q):
                        sp.dma_start(xb[:, par, :, q * CH:(q + 1) * CH], x_rows[b, :, :, q * CH:(q + 1) * CH]
                                     ).then_inc(s_x_in[par][q], 16)

                    for i, t in enumerate((wq, wk, wv, wskip)):
                        sp.dma_start(w_nat[:, i, :, :], t.rearrange("(t p) c -> p t c", p=P)).then_inc(s_w_in, 16)
                    sp.dma_start(ctxr[:, :, :], ctx_rows[0, :, :, :]).then_inc(s_ctx_in, 16)
                    for q in range(NQ):
                        load_x(0, 0, q)
                    sp.dma_start(gates[:, 0:1], g_xattn.rearrange("(a n) -> a n", a=1).to_broadcast([P, 1])
                                 ).then_inc(s_gates_in, 16)
                    sp.dma_start(gates[:, 1:2], g_ffn.rearrange("(a n) -> a n", a=1).to_broadcast([P, 1])
                                 ).then_inc(s_gates_in, 16)
                    sp.dma_start(biasg[:, :], bias.rearrange("(a n) -> a n", a=1).to_broadcast([P, O])
                                 ).then_inc(s_bias_in, 16)

                    sp.dma_start(a_nat, lora_a.rearrange("n r d -> (n r) d")).then_inc(s_lora_in, 16)
                    for n in range(NADAPT):
                        sp.dma_start(coef[n * RANK:(n + 1) * RANK, :],
                                     lora_weights[n:n + 1].rearrange("(a n) -> a n", a=1).to_broadcast([RANK, 1])
                                     ).then_inc(s_lora_in, 16)
                    load_w_block(sp, 0)
                    load_w_block(sp, 1)
                    for n in range(NADAPT):
                        sp.dma_start(b_nat[:, :, n, :], lora_b[n].rearrange("(p t) r -> p t r", p=P)
                                     ).then_inc(s_lora_in, 16)

                    def emit(b, par, first, last):
                        if not last:
                            sp.wait_ge(s_ctxl, b + 1)
                            sp.dma_start(ctxr[:, :, :], ctx_rows[b + 1, :, :, :]).then_inc(s_ctx_in, 16)
                        for q in range(NQ):
                            if not first and q >= 2:
                                for ct in range(CT):
                                    store_x1(b - 1, 1 - par, q, ct, XPB * (b - 1) + CT * q + ct)
                            if not last:
                                if not first:
                                    sp.wait_ge(s_x1_stored[q], 16 * CT * b)
                                load_x(b + 1, 1 - par, q)
                        for q in range(2):
                            for ct in range(CT):
                                store_x1(b, par, q, ct, XPB * b + CT * q + ct)

                    batches(emit, sp)
                    for q in (2, 3):
                        for ct in range(CT):
                            store_x1(B - 1, (B - 1) % 2, q, ct, XPB * (B - 1) + CT * q + ct)
                    for q in range(NQ):
                        sp.wait_ge(s_x1_stored[q], 16 * CT * B)

                @block.gpsimd
                def _(pool):
                    nc.gpsimd.memset(ident[:, :], 0.0).then_inc(s_ident0, 1)
                    nc.gpsimd.memset(minus_half[:, :], -0.5).then_inc(s_half, 1)
                    pool.wait_ge(s_ident0, 1)
                    nc.gpsimd.affine_select(out=ident[:, :], in_=ident[:, :], compare_op=ALU.not_equal, fill=1.0,
                                            base=0, pattern=[[-1, P]], channel_multiplier=1).then_inc(s_ident, 1)
                    def rstd_of(b, par):
                        pool.wait_ge(s_vare, b + 1)
                        nc.gpsimd.tensor_tensor(rstd[:, par, :], vare[:, :], minus_half[:, 0:CT],
                                                ALU.pow).then_inc(s_rstd, 1)

                    def u_low(b, q):
                        for ct in range(CT):
                            pool.wait_ge(s_uh, 8 * b + 2 * q + ct + 1)
                            cols = slice(q * CH, (q + 1) * CH)
                            nc.gpsimd.tensor_tensor(ul[:, ct, cols], u32[:, ct, :], uh[:, ct, cols],
                                                    ALU.subtract).then_inc(s_ul, 1)

                    def ctx_max(b):
                        pool.wait_ge(s_cmax, b + 1)
                        nc.gpsimd.tensor_tensor(idle_pool[:, :], minus_half[:, 0:1], minus_half[:, 1:2], ALU.add)
                        nc.gpsimd.partition_all_reduce(cmaxa[:, :], cmax[:, :], P, RMAX).then_inc(s_cmaxa, 1)

                    pool.wait_ge(s_half, 1)
                    ctx_max(0)
                    rstd_of(0, 0)
                    pool.wait_ge(s_wmax, 3)
                    nc.gpsimd.partition_all_reduce(wmaxa[:, :], wmax[:, :], P, RMAX).then_inc(s_wmaxa, 1)
                    u_low(0, 0)
                    u_low(0, 1)

                    def emit(b, par, first, last):
                        if not last:
                            ctx_max(b + 1)
                        u_low(b, 2)
                        u_low(b, 3)
                        if not last:
                            rstd_of(b + 1, 1 - par)
                            u_low(b + 1, 0)
                            u_low(b + 1, 1)

                    batches(emit, pool)

                @block.scalar
                def _(act):
                    act.wait_ge(s_gates_in, 32)
                    nc.scalar.activation(tg[:, :], gates[:, :], ACT.Tanh).then_inc(s_tanh, 1)

                    def ctx_high(b):
                        act.wait_ge(s_csc, 4 * b + 4)
                        nc.scalar.activation(ctxh[:, :, :], ctxr[:, :, :], ACT.Copy,
                                             scale=cscale[:, 0:1]).then_inc(s_ctxh, 1)

                    def gv_high(b, par, k):
                        act.wait_ge(s_gv_ps, 4 * b + k + 1)
                        dst = gh[:, par, k, :] if k < 2 else \
                            vh[:, par, 2 * k - 4:2 * k - 2, :].rearrange("p t c -> p (t c)")
                        nc.scalar.activation(dst, ps_gv[k][:, :], ACT.Copy, scale=2.0 ** GV_EXP).then_inc(s_gvh, 1)

                    def u_high(b, q, free):
                        if free is not None:
                            act.wait_ge(s_skip, free)
                        for ct in range(CT):
                            act.wait_ge(s_u32, 8 * b + 2 * q + ct + 1)
                            nc.scalar.activation(uh[:, ct, q * CH:(q + 1) * CH], u32[:, ct, :],
                                                 ACT.Copy).then_inc(s_uh, 1)

                    ctx_high(0)
                    act.wait_ge(s_wsc, 4)
                    for i in range(3):
                        nc.scalar.activation(wth[:, i, :, :], wt32[:, i, :, :], ACT.Copy,
                                             scale=wscale[:, i:i + 1]).then_inc(s_wth, 1)
                    u_high(0, 0, None)
                    for k in range(4):
                        gv_high(0, 0, k)
                    u_high(0, 1, None)

                    def exp_tile(b, par, s, first):
                        j = TPB * b + s
                        act.wait_ge(s_nbias, j + 1)
                        if not (first and s < 4):
                            act.wait_ge(s_t, j - 3)
                        nc.scalar.activation(pf[:, s % 4, :], ps_e[s % 2][:, :], ACT.Exp,
                                             bias=nbias[:, s % 4:s % 4 + 1], scale=e_scale[:, par:par + 1],
                                             accum_out=rsum[:, s % 4:s % 4 + 1]).then_inc(s_exp, 1)

                    def p_high(j, s):
                        act.wait_ge(s_t, j + 1)
                        nc.scalar.activation(pth[:, (s // TPC) % 2, :, (s % TPC) * P:(s % TPC + 1) * P],
                                             ps_t[s % 2][:, :].rearrange("p (t n) -> p t n", t=MT),
                                             ACT.Copy, scale=2.0 ** P_EXP).then_inc(s_pth, 1)

                    def p_normalise(j, s):
                        act.wait_ge(s_rinv, j + 1)
                        nc.scalar.activation(pf[:, s % 4, :], pf[:, s % 4, :], ACT.Copy,
                                             scale=rinv[:, s % 4:s % 4 + 1]).then_inc(s_pn, 1)

                    def load_piece(n, i):
                        act.dma_start(wscan[:, i, :], w_pieces[n, :, :]).then_inc(s_scan_in[i], 16)

                    def scan(b, i, final):
                        n = SPB * b + i
                        if not final:
                            if not (isinstance(n, int) and n == 0):
                                act.wait_ge(s_scanned, n)
                            load_piece(n + 1, 1 - i)
                        act.wait_ge(s_scan_in[i], 16 * (b + 1))
                        nc.scalar.activation(wjunk[:, :], wscan[:, i, :], ACT.Abs,
                                             accum_out=wabs[:, bass.ds(n, 1)]).then_inc(s_scanned, 1)

                    load_piece(0, 0)

                    def emit(b, par, first, last):
                        for s in range(TPB):
                            if not last and s - 1 in GV:
                                gv_high(b + 1, 1 - par, GV[s - 1])
                            exp_tile(b, par, s, first)
                            if not (first and s < 1):
                                p_normalise(TPB * b + s - 1, (s - 1) % TPB)
                            if not (first and s < 2):
                                p_high(TPB * b + s - 2, (s - 2) % TPB)
                            if s == 2:
                                u_high(b, 2, None if first else XPB * b - 2)
                            if s == 6:
                                u_high(b, 3, None if first else XPB * b)
                            if not last and s == 5:
                                ctx_high(b + 1)
                            if not last and s == 13:
                                u_high(b + 1, 0, XPB * b + 2)
                            if not last and s == 14:
                                u_high(b + 1, 1, XPB * b + 4)
                            if s in (4, 11):
                                scan(b, 0 if s == 4 else 1, last and s == 11)

                    batches(emit, act)
                    p_normalise(TPB * B - 1, TPB - 1)
                    for s in (TPB - 2, TPB - 1):
                        p_high(TPB * (B - 1) + s, s)

                @block.vector
                def _(dve):
                    def stats_of(b, par, q, ct):
                        if ct == 0:
                            dve.wait_ge(s_x_in[par][q], 8 * (b - par) + 16)
                        nc.vector.bn_stats(stats[:, ct, q, :], xb[:, par, ct, q * CH:(q + 1) * CH]
                                           ).then_inc(s_stats, 1)

                    def aggregate(b, par):
                        dve.wait_ge(s_stats, 8 * (b + 1))
                        nc.vector.tensor_copy(idle_dve[:, :], minus_half[:, 0:1])
                        for ct in range(CT):
                            nc.vector.bn_aggr(mv[:, ct, :], stats[:, ct, :, :].rearrange("p q s -> p (q s)")
                                              ).then_inc(s_aggr, 1)
                        dve.wait_ge(s_aggr, 2 * (b + 1))
                        nc.vector.tensor_copy(mean[:, par, :], mv[:, :, 0]).then_inc(s_mean, 1)
                        nc.vector.tensor_scalar(vare[:, :], mv[:, :, 1], EPS, 2.0 ** (-2 * U_EXP),
                                                ALU.add, ALU.mult).then_inc(s_vare, 1)

                    def normalise(b, par, q):
                        if q == 0:
                            dve.wait_ge(s_rstd, b + 1)
                            dve.wait_ge(s_mean, b + 1)
                        for ct in range(CT):
                            n = 8 * b + 2 * q + ct
                            if not (isinstance(n, int) and n < 2):
                                dve.wait_ge(s_ul, n - 1)
                            nc.vector.tensor_scalar(u32[:, ct, :], xb[:, par, ct, q * CH:(q + 1) * CH],
                                                    mean[:, par, ct:ct + 1], rstd[:, par, ct:ct + 1],
                                                    ALU.subtract, ALU.mult).then_inc(s_u32, 1)

                    def ctx_absmax(b):
                        dve.wait_ge(s_ctx_in, 16 * (b + 1))
                        nc.vector.tensor_reduce(cmax[:, :], ctxr[:, :, :], AX.XY, ALU.max,
                                                apply_absolute_value=True).then_inc(s_cmax, 1)

                    def power_of_two(dst, rec, scale, src, exponent, sem_, base):
                        nc.vector.tensor_scalar(rec, src, TINY, None, ALU.max).then_inc(sem_, 1)
                        dve.wait_ge(sem_, base + 1)
                        nc.vector.tensor_scalar(dst.bitcast(U32), rec.bitcast(U32), EXPONENT, None,
                                                ALU.bitwise_and).then_inc(sem_, 1)
                        dve.wait_ge(sem_, base + 2)
                        nc.vector.reciprocal(rec, dst).then_inc(sem_, 1)
                        dve.wait_ge(sem_, base + 3)
                        nc.vector.tensor_scalar(scale, rec, 2.0 ** exponent, None, ALU.mult).then_inc(sem_, 1)

                    def ctx_scale(b, par):
                        dve.wait_ge(s_cmaxa, b + 1)
                        power_of_two(cpow[:, :], crec[:, :], cscale[:, :], cmaxa[:, :], IN_EXP, s_csc, 4 * b)
                        nc.vector.tensor_tensor(e_scale[:, par:par + 1], cpow[:, :], c_exp[:, :], ALU.mult
                                                ).then_inc(s_escale, 1)

                    def attention_scale(b, par):
                        dve.wait_ge(s_csc, 4 * b + 2)
                        nc.vector.tensor_tensor(a_att[:, par:par + 1], cpow[:, :], c_att[:, :], ALU.mult
                                                ).then_inc(s_a_att, 1)

                    def ctx_low(b):
                        dve.wait_ge(s_ctxh, b + 1)
                        dve.wait_ge(s_csc, 4 * b + 4)
                        nc.vector.scalar_tensor_tensor(
                            out=ctxl[:, :, :].rearrange("p t m -> p (t m)"), in0=ctxr[:, :, :].rearrange("p t m -> p (t m)"),
                            scalar=cscale[:, 0:1], in1=ctxh[:, :, :].rearrange("p t m -> p (t m)"),
                            op0=ALU.mult, op1=ALU.subtract).then_inc(s_ctxl, 1)

                    def gv_low(b, par, k):
                        dve.wait_ge(s_gvh, 4 * b + k + 1)
                        dst, hi = (gl[:, par, k, :], gh[:, par, k, :]) if k < 2 else \
                            (vl[:, par, 2 * k - 4:2 * k - 2, :].rearrange("p t c -> p (t c)"),
                             vh[:, par, 2 * k - 4:2 * k - 2, :].rearrange("p t c -> p (t c)"))
                        nc.vector.scalar_tensor_tensor(out=dst, in0=ps_gv[k][:, :], scalar=2.0 ** GV_EXP, in1=hi,
                                                       op0=ALU.mult, op1=ALU.subtract).then_inc(s_gv, 1)

                    def row_max(b, par, s):
                        j = TPB * b + s
                        dve.wait_ge(s_energy, j + 1)
                        nc.vector.tensor_reduce(nmax[:, s % 4:s % 4 + 1], ps_e[s % 2][:, :], AX.X, ALU.max,
                                                negate=True).then_inc(s_nmax, 1)
                        if s == 0:
                            dve.wait_ge(s_escale, b + 1)
                        dve.wait_ge(s_nmax, j + 1)
                        nc.vector.tensor_tensor(nbias[:, s % 4:s % 4 + 1], nmax[:, s % 4:s % 4 + 1],
                                                e_scale[:, par:par + 1], ALU.mult).then_inc(s_nbias, 1)

                    def row_sum(j, s):
                        dve.wait_ge(s_exp, j + 1)
                        nc.vector.reciprocal(rinv[:, s % 4:s % 4 + 1], rsum[:, s % 4:s % 4 + 1]).then_inc(s_rinv, 1)

                    def p_low(j, s):
                        dve.wait_ge(s_pth, j + 1)
                        cols = slice((s % TPC) * P, (s % TPC + 1) * P)
                        nc.vector.scalar_tensor_tensor(out=ptl[:, (s // TPC) % 2, :, cols],
                                                       in0=ps_t[s % 2][:, :].rearrange("p (t n) -> p t n", t=MT),
                                                       scalar=2.0 ** P_EXP, in1=pth[:, (s // TPC) % 2, :, cols],
                                                       op0=ALU.mult, op1=ALU.subtract).then_inc(s_ptl, 1)

                    def add_piece(what):
                        b, par, q, ct, is_att = what
                        x1 = xb[:, par, ct, q * CH:(q + 1) * CH]
                        n = XPB * b + CT * q + ct
                        if not is_att:
                            dve.wait_ge(s_skip, n + 1)
                            nc.vector.scalar_tensor_tensor(out=x1, in0=ps_s[ct][:, :], scalar=a_skip[:, 0:1],
                                                           in1=x1, op0=ALU.mult, op1=ALU.add).then_inc(s_skip_add, 1)
                        else:
                            dve.wait_ge(s_att, n + 1)
                            dve.wait_ge(s_skip_add, n + 1)
                            if q == 0 and ct == 0:
                                dve.wait_ge(s_a_att, b + 1)
                            nc.vector.scalar_tensor_tensor(out=x1, in0=ps_a[ct][:, :], scalar=a_att[:, par:par + 1],
                                                           in1=x1, op0=ALU.mult, op1=ALU.add).then_inc(s_x1, 1)

                    dve.wait_ge(s_half, 1)
                    ctx_absmax(0)
                    for q in range(NQ):
                        for ct in range(CT):
                            stats_of(0, 0, q, ct)
                    aggregate(0, 0)
                    for i in range(3):
                        dve.wait_ge(s_wt_ps, i + 1)
                        for k in range(CT):
                            nc.vector.tensor_copy(wt32[:, i, k, :], ps_gv[2 * (i % 2) + k][:, 0:C]).then_inc(s_wt32, 1)
                        dve.wait_ge(s_wt32, 2 * i + 2)
                        nc.vector.tensor_reduce(wmax[:, i:i + 1], wt32[:, i, :, :], AX.XY, ALU.max,
                                                apply_absolute_value=True).then_inc(s_wmax, 1)
                    dve.wait_ge(s_wmaxa, 1)
                    power_of_two(wpow[:, :], wrec[:, :], wscale[:, :], wmaxa[:, :], IN_EXP, s_wsc, 0)
                    dve.wait_ge(s_wsc, 4)
                    nc.vector.tensor_scalar(c_exp[:, :], wpow[:, 0:1], 2.0 ** (-4 - U_EXP - GV_EXP - 2 * IN_EXP),
                                            None, ALU.mult).then_inc(s_wsc, 1)
                    dve.wait_ge(s_tanh, 1)
                    nc.vector.tensor_scalar(c_att[:, :], wpow[:, 1:2], tg[:, 0:1],
                                            2.0 ** (-P_EXP - GV_EXP - 2 * IN_EXP), ALU.mult, ALU.mult
                                            ).then_inc(s_wsc, 1)
                    nc.vector.tensor_scalar(a_skip[:, :], wpow[:, 2:3], tg[:, 0:1],
                                            2.0 ** (-U_EXP - IN_EXP), ALU.mult, ALU.mult).then_inc(s_wsc, 1)
                    dve.wait_ge(s_wsc, 7)
                    ctx_scale(0, 0)
                    attention_scale(0, 0)
                    ctx_low(0)
                    for i in range(3):
                        dve.wait_ge(s_wth, i + 1)
                        nc.vector.scalar_tensor_tensor(
                            out=wtl[:, i, :, :].rearrange("p t c -> p (t c)"),
                            in0=wt32[:, i, :, :].rearrange("p t c -> p (t c)"), scalar=wscale[:, i:i + 1],
                            in1=wth[:, i, :, :].rearrange("p t c -> p (t c)"),
                            op0=ALU.mult, op1=ALU.subtract).then_inc(s_wtl, 1)
                    normalise(0, 0, 0)
                    for k in range(4):
                        gv_low(0, 0, k)
                    normalise(0, 0, 1)
                    dve.wait_ge(s_bias_in, 16)
                    nc.vector.tensor_scalar(biasg[:, :], biasg[:, :], tg[:, 1:2], None, ALU.mult).then_inc(s_biasg, 1)

                    def emit(b, par, first, last):
                        for s in range(TPB):
                            j = TPB * b + s
                            if not last and s - 1 in GV:
                                gv_low(b + 1, 1 - par, GV[s - 1])
                            row_max(b, par, s)
                            if not (first and s < 1):
                                row_sum(j - 1, (s - 1) % TPB)
                            if not (first and s < 3):
                                p_low(j - 3, (s - 3) % TPB)
                            if s > 0 and piece(b, par, s - 1, first):
                                add_piece(piece(b, par, s - 1, first))
                            elif s == 0 and not first:
                                add_piece(piece(b - 1, 1 - par, TPB - 1, False))
                            if s == 2:
                                normalise(b, par, 2)
                            if s == 6:
                                normalise(b, par, 3)
                            if not last:
                                if s == 2:
                                    ctx_absmax(b + 1)
                                if s == 4:
                                    ctx_scale(b + 1, 1 - par)
                                if s == 5:
                                    ctx_low(b + 1)
                                if s == LAG + 1:
                                    attention_scale(b + 1, 1 - par)
                                if s in STATS:
                                    stats_of(b + 1, 1 - par, STATS[s], 0)
                                    stats_of(b + 1, 1 - par, STATS[s], 1)
                                if s == 12:
                                    aggregate(b + 1, 1 - par)
                                if s == 13:
                                    normalise(b + 1, 1 - par, 0)
                                if s == 14:
                                    normalise(b + 1, 1 - par, 1)

                    STATS = {3: 0, 6: 1, 9: 2, 11: 3}
                    batches(emit, dve)
                    row_sum(TPB * B - 1, TPB - 1)
                    for s in (TPB - 3, TPB - 2, TPB - 1):
                        p_low(TPB * (B - 1) + s, s)
                    add_piece(piece(B - 1, (B - 1) % 2, TPB - 1, False))
                    for s in range(LAG):
                        add_piece(piece(B, B % 2, s, False))

                @block.tensor
                def _(pe):
                    def split_product(dst, terms, finish):
                        ops = [(lo_l if k == 2 else hi_l, lo_r if k == 1 else hi_r)
                               for (hi_l, lo_l), (hi_r, lo_r) in terms for k in range(3)]
                        for n, (lhs, rhs) in enumerate(ops):
                            ins = nc.tensor.matmul(dst, lhs, rhs, start=n == 0, stop=n == len(ops) - 1)
                        if finish is not None:
                            ins.then_inc(finish, 1)

                    pe.wait_ge(s_w_in, 64)
                    for k in range(CT):
                        for o in range(CT):
                            ins = nc.tensor.matmul(ps_gv[k][:, 0:C], w_nat[:, 1, o, k * P:(k + 1) * P],
                                                   w_nat[:, 0, o, :], start=o == 0, stop=o == CT - 1)
                    ins.then_inc(s_wt_ps, 1)
                    pe.wait_ge(s_ident, 1)
                    for i in (1, 2):
                        if i == 2:
                            pe.wait_ge(s_wt32, 2)
                        for k in range(CT):
                            for o in range(CT):
                                ins = nc.tensor.transpose(ps_gv[2 * (i % 2) + k][:, o * P:(o + 1) * P],
                                                          w_nat[:, i + 1, o, k * P:(k + 1) * P], ident[:, :])
                        ins.then_inc(s_wt_ps, 1)

                    def g_or_v(b, par, k):
                        if k == 0:
                            pe.wait_ge(s_ctxl, b + 1)
                        if k < 2:
                            rows = slice(k * P, (k + 1) * P)
                            split_product(ps_gv[k][:, :],
                                          [((wth[:, 0, t, rows], wtl[:, 0, t, rows]), (ctxh[:, t, :], ctxl[:, t, :]))
                                           for t in range(CT)], s_gv_ps)
                        else:
                            for i in range(2):
                                rows = slice((2 * k - 4 + i) * P, (2 * k - 3 + i) * P)
                                split_product(ps_gv[k][:, i * C:(i + 1) * C],
                                              [((ctxh[:, t, rows], ctxl[:, t, rows]), (wth[:, 1, t, :], wtl[:, 1, t, :]))
                                               for t in range(CT)], s_gv_ps if i else None)

                    pe.wait_ge(s_wtl, 3)
                    for k in range(4):
                        g_or_v(0, 0, k)

                    def energy(b, par, s, first):
                        j = TPB * b + s
                        if s % TPC == 0:
                            pe.wait_ge(s_ul, 8 * b + 2 * (s // TPC) + 2)
                        if s == 0:
                            pe.wait_ge(s_gv, 4 * b + 2)
                        if not (first and s < 2):
                            pe.wait_ge(s_exp, j - 1)
                        split_product(ps_e[s % 2][:, :],
                                      [((uh[:, k, s * P:(s + 1) * P], ul[:, k, s * P:(s + 1) * P]),
                                        (gh[:, par, k, :], gl[:, par, k, :])) for k in range(CT)], s_energy)

                    def transpose_p(j, s):
                        pe.wait_ge(s_pn, j + 1)
                        if not (isinstance(j, int) and j < 2):
                            pe.wait_ge(s_ptl, j - 1)
                        for mt in range(MT):
                            ins = nc.tensor.transpose(ps_t[s % 2][:, mt * P:(mt + 1) * P],
                                                      pf[:, s % 4, mt * P:(mt + 1) * P], ident[:, :])
                        ins.then_inc(s_t, 1)

                    def sum_piece(what, first, last):
                        b, par, q, ct, is_att = what
                        n = XPB * b + CT * q + ct
                        cols = slice(q * CH, (q + 1) * CH)
                        rows = slice(ct * P, (ct + 1) * P)
                        k = 2 * ct + is_att
                        if q == 0 and first:
                            pe.wait_ge(s_gv, k + 1)
                        elif q == 1 and not last:
                            pe.wait_ge(s_gv, 4 * (b + 1) + k + 1)
                        else:
                            pe.wait_ge(s_x1 if is_att else s_skip_add, n - 1)
                        if not is_att:
                            split_product(ps_s[ct][:, :],
                                          [((wth[:, 2, t, rows], wtl[:, 2, t, rows]), (uh[:, t, cols], ul[:, t, cols]))
                                           for t in range(CT)], s_skip)
                            return
                        if ct == 0:
                            pe.wait_ge(s_ptl, TPB * b + TPC * (q + 1))
                            if q == 0:
                                pe.wait_ge(s_gv, 4 * b + 4)
                        split_product(ps_a[ct][:, :],
                                      [((vh[:, par, m, rows], vl[:, par, m, rows]),
                                        (pth[:, q % 2, m, :], ptl[:, q % 2, m, :])) for m in range(MT)], s_att)

                    def emit(b, par, first, last):
                        for s in range(TPB):
                            energy(b, par, s, first)
                            if not last and s in GV:
                                k = GV[s]
                                pe.wait_ge(s_x1 if k % 2 else s_skip_add, XPB * b + k // 2 + 1)
                                g_or_v(b + 1, 1 - par, k)
                            if piece(b, par, s, first):
                                sum_piece(piece(b, par, s, first), first, last)
                            if not (first and s < 2):
                                transpose_p(TPB * b + s - 2, (s - 2) % TPB)

                    batches(emit, pe)
                    for s in range(LAG):
                        sum_piece(piece(B, B % 2, s, False), False, False)
                        if s < 2:
                            transpose_p(TPB * B + s - 2, TPB + s - 2)

        with ExitStack() as phase:
            def sb(name, shape, dt):
                return phase.enter_context(nc.sbuf_tensor(name, shape, dt))

            def ps(name):
                return phase.enter_context(nc.psum_tensor(name, [P, CH], F32))

            wh = sb("wh", [P, OC * KT, CH], F16)
            wl = sb("wl", [P, OC * KT, CH], F16)
            u2h = sb("u2h", [P, 2, KT, P], F16)
            u2l = sb("u2l", [P, 2, KT, P], F16)
            fmax = sb("fmax", [P, 3], F32)
            fmaxa = sb("fmaxa", [P, 3], F32)
            fbound = sb("fbound", [P, 2], F32)
            fpow = sb("fpow", [P, 1], F32)
            frec = sb("frec", [P, 1], F32)
            fscale = sb("fscale", [P, 1], F32)
            a_ffn = sb("a_ffn", [P, 1], F32)
            stats2 = sb("stats2", [P, 4, 6], F32)
            mv2 = sb("mv2", [P, 2], F32)
            vare2 = sb("vare2", [P, 1], F32)
            rstd2 = sb("rstd2", [P, 1], F32)

            ps_w = [ps(f"ps_w{i}") for i in range(4)]
            ps_u = [ps("ps_u0"), ps("ps_u1")]
            ps_f = [ps("ps_f0"), ps("ps_f1")]

            s_bt_ps = sem("s_bt_ps")
            s_bt = sem("s_bt")
            s_fmax = sem("s_fmax")
            s_fmaxa = sem("s_fmaxa")
            s_fsc = sem("s_fsc")
            s_unit = sem("s_unit")
            s_wh = sem("s_wh")
            s_wl = sem("s_wl")
            s_row_in = [sem(f"s_row_in{i}") for i in range(4)]
            s_out_stored = sem("s_out_stored")
            s_stats2 = sem("s_stats2")
            s_aggr2 = sem("s_aggr2")
            s_vare2 = sem("s_vare2")
            s_rstd2 = sem("s_rstd2")
            s_u2 = sem("s_u2")
            s_xbias = sem("s_xbias")
            s_ut = sem("s_ut")
            s_u2h = sem("s_u2h")
            s_u2l = sem("s_u2l")
            s_f = sem("s_f")
            s_out = sem("s_out")

            def row_tiles(emit, eng):
                for r in range(4):
                    emit(r, 0, r, r == 0, False)
                with eng.Fori(1, ST // 4 - 1) as i:
                    for r in range(4):
                        emit(4 * i + r, i, r, False, False)
                for r in range(4):
                    emit(ST - 4 + r, ST // 4 - 1, r, False, r == 3)

            with nc.Block() as block:

                @block.sync
                def _(sp):
                    def load_row(i, r):
                        sp.dma_start(xring[:, r, :], x1_tiles[i, :, :]).then_inc(s_row_in[r], 16)

                    load_row(0, 0)
                    for blk in range(2, 16):
                        sp.wait_ge(s_unit, 4 * (blk - 1))
                        load_w_block(sp, blk)
                    sp.wait_ge(s_unit, OC * KT)
                    load_row(1, 1)
                    load_row(2, 2)

                    def emit(i, f, r, first, last):
                        if not (isinstance(i, int) and i + 3 >= ST):
                            if not first:
                                sp.wait_ge(s_out_stored, 16 * i)
                            load_row(i + 3, (r + 3) % 4)
                        if last:
                            for oc in range(OC):
                                sp.wait_ge(s_out, OC * i + oc + 1)
                                sp.dma_start(out_tiles[i, :, oc * CH:(oc + 1) * CH],
                                             xring[:, r, oc * CH:(oc + 1) * CH]).then_inc(s_out_stored, 16)
                        else:
                            sp.wait_ge(s_out, OC * (i + 1))
                            sp.dma_start(out_tiles[i, :, :], xring[:, r, :]).then_inc(s_out_stored, 16)

                    row_tiles(emit, sp)
                    sp.wait_ge(s_out_stored, 16 * (ST - 1 + OC))

                @block.gpsimd
                def _(pool):
                    pool.wait_ge(s_fmax, 3)
                    nc.gpsimd.partition_all_reduce(fmaxa[:, :], fmax[:, :], P, RMAX).then_inc(s_fmaxa, 1)

                    def prepare(i, r):
                        pool.wait_ge(s_vare2, i + 1)
                        nc.gpsimd.tensor_tensor(rstd2[:, :], vare2[:, :], minus_half[:, 0:1],
                                                ALU.pow).then_inc(s_rstd2, 1)
                        pool.wait_ge(s_u2, i + 1)
                        nc.gpsimd.tensor_tensor(xring[:, r, :], xring[:, r, :], biasg[:, :],
                                                ALU.add).then_inc(s_xbias, 1)

                    def emit(i, f, r, first, last):
                        if not last:
                            prepare(i + 1, (r + 1) % 4)

                    prepare(0, 0)
                    row_tiles(emit, pool)

                @block.scalar
                def _(act):
                    act.wait_ge(s_fsc, 7)

                    with act.Fori(0, OC) as oc:
                        for kt in range(KT):
                            act.wait_ge(s_unit, KT * oc + kt + 1)
                            nc.scalar.activation(wh[:, bass.ds(KT * oc + kt, 1), :], ps_w[kt % 4][:, None, :],
                                                 ACT.Copy, scale=fscale[:, 0:1]).then_inc(s_wh, 1)

                    def u2_high(i, r):
                        for k in range(4):
                            act.wait_ge(s_ut, 4 * i + k + 1)
                            nc.scalar.activation(u2h[:, r % 2, 4 * k:4 * k + 4, :].rearrange("p t n -> p (t n)"),
                                                 ps_u[k % 2][:, :], ACT.Copy).then_inc(s_u2h, 1)

                    def emit(i, f, r, first, last):
                        if not last:
                            u2_high(i + 1, r + 1)

                    u2_high(0, 0)
                    row_tiles(emit, act)

                @block.vector
                def _(dve):
                    dve.wait_ge(s_lora_in, 16 * (1 + 2 * NADAPT))
                    for g in range(4):
                        dve.wait_ge(s_bt_ps, g + 1)
                        nc.vector.tensor_scalar(
                            bt[:, :].rearrange("q (p t) -> q t p", t=KT)[:, 4 * g:4 * g + 4, :],
                            ps_w[g][:, :].rearrange("q (t p) -> q t p", t=4), coef[:, 0:1], LORA_SCALE,
                            ALU.mult, ALU.mult).then_inc(s_bt, 1)
                    nc.vector.tensor_reduce(fmax[:, 0:1], a_nat, AX.X, ALU.max,
                                            apply_absolute_value=True).then_inc(s_fmax, 1)
                    nc.vector.tensor_reduce(fmax[:, 2:3], wabs[:, :], AX.X, ALU.max).then_inc(s_fmax, 1)
                    dve.wait_ge(s_bt, 4)
                    nc.vector.tensor_reduce(fmax[:, 1:2], bt[:, :], AX.X, ALU.max,
                                            apply_absolute_value=True).then_inc(s_fmax, 1)
                    dve.wait_ge(s_fmaxa, 1)
                    nc.vector.tensor_tensor(fbound[:, 0:1], fmaxa[:, 0:1], fmaxa[:, 1:2], ALU.mult).then_inc(s_fsc, 1)
                    dve.wait_ge(s_fsc, 1)
                    nc.vector.scalar_tensor_tensor(out=fbound[:, 1:2], in0=fbound[:, 0:1], scalar=float(P),
                                                   in1=fmaxa[:, 2:3], op0=ALU.mult, op1=ALU.add).then_inc(s_fsc, 1)
                    dve.wait_ge(s_fsc, 2)
                    nc.vector.tensor_scalar(frec[:, :], fbound[:, 1:2], TINY, None, ALU.max).then_inc(s_fsc, 1)
                    dve.wait_ge(s_fsc, 3)
                    nc.vector.tensor_scalar(fpow[:, :].bitcast(U32), frec[:, :].bitcast(U32), EXPONENT, None,
                                            ALU.bitwise_and).then_inc(s_fsc, 1)
                    dve.wait_ge(s_fsc, 4)
                    nc.vector.reciprocal(frec[:, :], fpow[:, :]).then_inc(s_fsc, 1)
                    nc.vector.tensor_scalar(a_ffn[:, :], fpow[:, :], tg[:, 1:2], 2.0 ** (-U_EXP - W_EXP),
                                            ALU.mult, ALU.mult).then_inc(s_fsc, 1)
                    dve.wait_ge(s_fsc, 6)
                    nc.vector.tensor_scalar(fscale[:, :], frec[:, :], 2.0 ** W_EXP, None, ALU.mult).then_inc(s_fsc, 1)
                    dve.wait_ge(s_fsc, 7)

                    def prepare(i, f, r):
                        dve.wait_ge(s_row_in[r], 16 * (f + 1))
                        for q in range(4):
                            nc.vector.bn_stats(stats2[:, q, :], xring[:, r, q * CH:(q + 1) * CH]).then_inc(s_stats2, 1)
                        dve.wait_ge(s_stats2, 4 * (i + 1))
                        nc.vector.tensor_copy(idle_dve[:, :], minus_half[:, 0:1])
                        nc.vector.bn_aggr(mv2[:, :], stats2[:, :, :].rearrange("p q s -> p (q s)")).then_inc(s_aggr2, 1)
                        dve.wait_ge(s_aggr2, i + 1)
                        nc.vector.tensor_scalar(vare2[:, :], mv2[:, 1:2], EPS, 2.0 ** (-2 * U_EXP),
                                                ALU.add, ALU.mult).then_inc(s_vare2, 1)
                        dve.wait_ge(s_rstd2, i + 1)
                        if not (isinstance(i, int) and i == 0):
                            dve.wait_ge(s_ut, 4 * i)
                        nc.vector.tensor_scalar(u2[:, :], xring[:, r, :], mv2[:, 0:1], rstd2[:, 0:1],
                                                ALU.subtract, ALU.mult).then_inc(s_u2, 1)

                    def u2_low(i, r, ks):
                        for k in ks:
                            dve.wait_ge(s_u2h, 4 * i + k + 1)
                            nc.vector.tensor_tensor(u2l[:, r % 2, 4 * k:4 * k + 4, :].rearrange("p t n -> p (t n)"),
                                                    ps_u[k % 2][:, :],
                                                    u2h[:, r % 2, 4 * k:4 * k + 4, :].rearrange("p t n -> p (t n)"),
                                                    ALU.subtract).then_inc(s_u2l, 1)

                    def finish(i, r, oc):
                        dve.wait_ge(s_f, OC * i + oc + 1)
                        if oc == 0:
                            dve.wait_ge(s_xbias, i + 1)
                        o = xring[:, r, oc * CH:(oc + 1) * CH]
                        nc.vector.scalar_tensor_tensor(out=o, in0=ps_f[oc % 2][:, :], scalar=a_ffn[:, 0:1], in1=o,
                                                       op0=ALU.mult, op1=ALU.add).then_inc(s_out, 1)

                    prepare(0, 0, 0)
                    with dve.Fori(0, OC) as oc:
                        for kt in range(KT):
                            dve.wait_ge(s_wh, KT * oc + kt + 1)
                            n = bass.ds(KT * oc + kt, 1)
                            nc.vector.scalar_tensor_tensor(
                                out=wl[:, n, :], in0=ps_w[kt % 4][:, None, :], scalar=fscale[:, 0:1],
                                in1=wh[:, n, :], op0=ALU.mult, op1=ALU.subtract).then_inc(s_wl, 1)
                    u2_low(0, 0, range(4))

                    def emit(i, f, r, first, last):
                        if not last:
                            prepare(i + 1, f + (1 if r == 3 else 0), (r + 1) % 4)
                        finish(i, r, 0)
                        if not last:
                            u2_low(i + 1, r + 1, (0, 1))
                        finish(i, r, 1)
                        if not last:
                            u2_low(i + 1, r + 1, (2, 3))
                        finish(i, r, 2)
                        finish(i, r, 3)

                    row_tiles(emit, dve)

                @block.tensor
                def _(pe):
                    pe.wait_ge(s_lora_in, 16 * (1 + 2 * NADAPT))
                    for g in range(4):
                        for t in range(4):
                            ins = nc.tensor.transpose(ps_w[g][:, t * P:(t + 1) * P], b_nat[:, 4 * g + t, :, :].rearrange("p n r -> p (n r)"),
                                                      ident[:, :])
                        ins.then_inc(s_bt_ps, 1)
                    pe.wait_ge(s_bt, 4)

                    def unit(oc, kt):
                        if kt % 4 == 0:
                            pe.wait_ge(s_wstage[(kt // 4) % 2], 32 * oc + 16 * (kt // 8 + 1))
                        if not (isinstance(oc, int) and kt < 4):
                            pe.wait_ge(s_wl, KT * oc + kt - 3)
                        for t in range(4):
                            nc.tensor.matmul(ps_w[kt % 4][:, t * P:(t + 1) * P],
                                             w_stage[(kt // 4) % 2][:, t, (kt % 4) * P:(kt % 4 + 1) * P],
                                             ident[:, :], is_transpose=True, start=t == 0, stop=False)
                        nc.tensor.matmul(ps_w[kt % 4][:, :], a_nat[:, kt * P:(kt + 1) * P],
                                         bt[:, bass.ds(CH * oc, CH)], start=False, stop=True).then_inc(s_unit, 1)

                    for kt in range(KT):
                        unit(0, kt)
                    with pe.Fori(1, OC) as oc:
                        for kt in range(KT):
                            unit(oc, kt)

                    def transpose_rows(i, r, k):
                        n = 4 * i + k
                        if k == 0:
                            pe.wait_ge(s_u2, i + 1)
                        if not (isinstance(n, int) and n < 2):
                            pe.wait_ge(s_u2l, n - 1)
                        for t in range(4):
                            ins = nc.tensor.transpose(ps_u[k % 2][:, t * P:(t + 1) * P],
                                                      u2[:, (4 * k + t) * P:(4 * k + t + 1) * P], ident[:, :])
                        ins.then_inc(s_ut, 1)

                    def product(i, r, oc):
                        if oc == 0:
                            pe.wait_ge(s_u2l, 4 * (i + 1))
                        if isinstance(i, int) and i == 0:
                            pe.wait_ge(s_wl, KT * (oc + 1))
                        if not (isinstance(i, int) and i == 0 and oc < 2):
                            pe.wait_ge(s_out, OC * i + oc - 1)
                        for kt in range(KT):
                            hi, lo = u2h[:, r % 2, kt, :], u2l[:, r % 2, kt, :]
                            n = oc * KT + kt
                            nc.tensor.matmul(ps_f[oc % 2][:, :], hi, wh[:, n, :], start=kt == 0, stop=False)
                            nc.tensor.matmul(ps_f[oc % 2][:, :], hi, wl[:, n, :], start=False, stop=False)
                            ins = nc.tensor.matmul(ps_f[oc % 2][:, :], lo, wh[:, n, :], start=False,
                                                   stop=kt == KT - 1)
                        ins.then_inc(s_f, 1)

                    for k in range(4):
                        transpose_rows(0, 0, k)

                    def emit(i, f, r, first, last):
                        product(i, r, 0)
                        if not last:
                            transpose_rows(i + 1, r + 1, 0)
                            transpose_rows(i + 1, r + 1, 1)
                        product(i, r, 1)
                        if not last:
                            transpose_rows(i + 1, r + 1, 2)
                            transpose_rows(i + 1, r + 1, 3)
                        product(i, r, 2)
                        product(i, r, 3)

                    row_tiles(emit, pe)


_INS = ["x", "ctx_1024", "g_xattn", "g_ffn", "L0_xattn_Wq", "L0_xattn_Wk", "L0_xattn_Wv", "L0_xattn_Wskip",
        "L0_ffn_lora_A", "L0_ffn_lora_B", "L0_ffn_W", "L0_ffn_bias", "L0_ffn_lora_weights"]


def kernel(**inputs):
    import numpy as _np
    import concourse.bacc as _bacc
    from concourse import mybir as _mybir
    from concourse.bass_utils import run_bass_kernel_spmd as _run

    nc = _bacc.Bacc("TRN2", target_bir_lowering=False, num_devices=1)
    arrays, args = {}, []
    for name in _INS:
        a = _np.ascontiguousarray(inputs[name])
        arrays[f"in_{name}"] = a
        args.append(nc.dram_tensor(f"in_{name}", a.shape, _mybir.dt.from_np(a.dtype), kind="ExternalInput").ap())
    args.append(nc.dram_tensor("out_0", inputs["x"].shape, _mybir.dt.float32, kind="ExternalOutput").ap())
    flamingo_kernel(nc, *args)
    r = _run(nc, [arrays], core_ids=[0])
    return r.results[0]["out_0"]
```

```python
from contextlib import ExitStack

import concourse.bass as bass
from concourse import mybir

F32 = mybir.dt.float32
F16 = mybir.dt.float16
U32 = mybir.dt.uint32
ALU = mybir.AluOpType
ACT = mybir.ActivationFunctionType
AX = mybir.AxisListType
RMAX = bass.bass_isa.ReduceOp.max

P = 128
EXPONENT = 0x7F800000
TINY = 1e-30
EPS = 1e-5
U_EXP = 10
P_EXP = 14
IN_EXP = 6
GV_EXP = -7
W_EXP = 14
LORA_SCALE = 2.0


def flamingo_kernel(nc, x, ctx_in, g_xattn, g_ffn, wq, wk, wv, wskip, lora_a, lora_b, w, bias,
                    lora_weights, out):
    B, C, N = x.shape
    M = ctx_in.shape[2]
    NADAPT, RANK, D = lora_a.shape
    O = w.shape[0]
    CT = C // P
    MT = M // P
    CH = 512
    NQ = N // CH
    TPC = CH // P
    TPB = N // P
    KT = D // P
    OC = O // CH
    ST = B * C // P
    XPB = CT * NQ
    assert CT == 2 and MT == 4 and NQ == 4 and TPC == 4 and NADAPT * RANK == P

    x1_dram = nc.dram_tensor("x1_scratch", [B, C, N], F32, kind="Internal").ap()
    x_rows = x.rearrange("b (t p) n -> b p t n", p=P)
    x1_rows = x1_dram.rearrange("b (t p) n -> b p t n", p=P)
    x1_tiles = x1_dram.rearrange("b (t p) n -> (b t) p n", p=P)
    out_tiles = out.rearrange("b (t p) n -> (b t) p n", p=P)
    ctx_rows = ctx_in.rearrange("b (t p) m -> b p t m", p=P)

    with ExitStack() as outer:
        def sem(name):
            return outer.enter_context(nc.semaphore(name))

        def keep(name, shape, dt):
            return outer.enter_context(nc.sbuf_tensor(name, shape, dt))

        ident = keep("ident", [P, P], F32)
        xring = keep("xring", [P, 4, D], F32)
        u2 = keep("u2", [P, D], F32)
        bt = keep("bt", [P, O], F32)
        biasg = keep("biasg", [P, O], F32)
        tg = keep("tg", [P, 2], F32)
        coef = keep("coef", [P, 1], F32)
        wabs = keep("wabs", [P, O * D // (P * 1024)], F32)
        minus_half = keep("minus_half", [P, 2], F32)
        idle_pool = keep("idle_pool", [P, 1], F32)
        idle_dve = keep("idle_dve", [P, 1], F32)
        fscale = keep("fscale", [P, 1], F32)
        a_ffn = keep("a_ffn", [P, 1], F32)
        a_nat = xring[:, 1, :]
        w_stage = [t.rearrange("p (t d) -> p t d", t=4)
                   for t in (xring[:, 2, :], xring[:, 3, :], xring[:, 0, :], u2[:, :])]
        b_nat = u2[:, :].rearrange("p (t n r) -> p t n r", n=NADAPT, r=RANK)

        s_ident0 = sem("s_ident0")
        s_ident = sem("s_ident")
        s_lora_in = sem("s_lora_in")
        s_wstage = [sem(f"s_wstage{i}") for i in range(5)]

        def stage_of(blk):
            return blk % 4 if blk < 12 else (0, 1, 4, 0)[blk - 12]

        def load_w_block(eng, blk):
            oc, db = blk // 4, blk % 4
            src = w[oc * CH:(oc + 1) * CH, db * 512:(db + 1) * 512].rearrange("(t p) d -> p t d", p=P)
            eng.dma_start(w_stage[stage_of(blk)], src).then_inc(s_wstage[stage_of(blk)], 16)

        with ExitStack() as phase:
            def sb(name, shape, dt):
                return phase.enter_context(nc.sbuf_tensor(name, shape, dt))

            def ps(name):
                return phase.enter_context(nc.psum_tensor(name, [P, CH], F32))

            xb = sb("xb", [P, 2, CT, N], F32)
            uh = sb("uh", [P, CT, N], F16)
            ul = sb("ul", [P, CT, N], F16)
            u32 = sb("u32", [P, CT, CH], F32)
            pf = sb("pf", [P, 4, M], F32)
            pth = sb("pth", [P, 2, MT, CH], F16)
            ptl = sb("ptl", [P, 2, MT, CH], F16)
            ctxr = sb("ctxr", [P, CT, M], F32)
            ctxh = sb("ctxh", [P, CT, M], F16)
            ctxl = sb("ctxl", [P, CT, M], F16)
            gh = sb("gh", [P, 2, CT, M], F16)
            gl = sb("gl", [P, 2, CT, M], F16)
            vh = sb("vh", [P, 2, MT, C], F16)
            vl = sb("vl", [P, 2, MT, C], F16)
            w_nat = sb("w_nat", [P, 4, CT, C], F32)
            wth = sb("wth", [P, 3, CT, C], F16)
            wtl = sb("wtl", [P, 3, CT, C], F16)
            wscan = sb("wscan", [P, 2, 1024], F32)
            wjunk = sb("wjunk", [P, 1024], F32)
            gates = sb("gates", [P, 2], F32)
            wmax = sb("wmax", [P, 3], F32)
            wmaxa = sb("wmaxa", [P, 3], F32)
            wpow = sb("wpow", [P, 3], F32)
            wrec = sb("wrec", [P, 3], F32)
            wscale = sb("wscale", [P, 3], F32)
            c_exp = sb("c_exp", [P, 1], F32)
            c_att = sb("c_att", [P, 1], F32)
            a_skip = sb("a_skip", [P, 1], F32)
            cmax = sb("cmax", [P, 1], F32)
            cmaxa = sb("cmaxa", [P, 1], F32)
            cpow = sb("cpow", [P, 1], F32)
            crec = sb("crec", [P, 1], F32)
            cscale = sb("cscale", [P, 1], F32)
            e_scale = sb("e_scale", [P, 2], F32)
            a_att = sb("a_att", [P, 2], F32)
            fmax = sb("fmax", [P, 3], F32)
            fmaxa = sb("fmaxa", [P, 3], F32)
            fbound = sb("fbound", [P, 2], F32)
            fpow = sb("fpow", [P, 1], F32)
            frec = sb("frec", [P, 1], F32)
            nmax = sb("nmax", [P, 4], F32)
            nbias = sb("nbias", [P, 4], F32)
            rsum = sb("rsum", [P, 4], F32)
            rinv = sb("rinv", [P, 4], F32)
            stats = sb("stats", [P, CT, NQ, 6], F32)
            mv = sb("mv", [P, CT, 2], F32)
            vare = sb("vare", [P, CT], F32)
            rstd = sb("rstd", [P, 2, CT], F32)
            mean = sb("mean", [P, 2, CT], F32)

            ps_e = [ps("ps_e0"), ps("ps_e1")]
            ps_t = [ps("ps_t0"), ps("ps_t1")]
            ps_s = [ps("ps_s0"), ps("ps_s1")]
            ps_a = [ps("ps_a0"), ps("ps_a1")]
            ps_gv = [ps_s[0], ps_a[0], ps_s[1], ps_a[1]]
            ps_wt = [ps_t[0], ps_t[1], ps_e[1]]

            s_w_in = [sem("s_wqk_in"), sem("s_wvskip_in")]
            s_gates_in = sem("s_gates_in")
            s_tanh = sem("s_tanh")
            s_half = sem("s_half")
            s_bias_in = sem("s_bias_in")
            s_wt_ps = sem("s_wt_ps")
            s_wmax = sem("s_wmax")
            s_wmaxa = sem("s_wmaxa")
            s_wsc = sem("s_wsc")
            s_wth = sem("s_wth")
            s_wtl = sem("s_wtl")
            s_x_in = [[sem(f"s_x_in{i}{q}") for q in range(NQ)] for i in range(2)]
            s_ctx_in = sem("s_ctx_in")
            s_x1_stored = [sem(f"s_x1_stored{q}") for q in range(NQ)]
            s_scan_in = [sem("s_scan_in0"), sem("s_scan_in1")]
            s_scanned = sem("s_scanned")
            s_stats = sem("s_stats")
            s_aggr = sem("s_aggr")
            s_vare = sem("s_vare")
            s_rstd = sem("s_rstd")
            s_u32 = sem("s_u32")
            s_uh = sem("s_uh")
            s_ul = sem("s_ul")
            s_cmax = sem("s_cmax")
            s_cmaxa = sem("s_cmaxa")
            s_csc = sem("s_csc")
            s_ctxh = sem("s_ctxh")
            s_ctxl = sem("s_ctxl")
            s_gvh = sem("s_gvh")
            s_gv = sem("s_gv")
            s_fmax = sem("s_fmax")
            s_fmaxa = sem("s_fmaxa")
            s_fsc = sem("s_fsc")
            s_energy = sem("s_energy")
            s_nmax = sem("s_nmax")
            s_nbias = sem("s_nbias")
            s_exp = sem("s_exp")
            s_rinv = sem("s_rinv")
            s_pn = sem("s_pn")
            s_t = sem("s_t")
            s_pth = sem("s_pth")
            s_ptl = sem("s_ptl")
            s_skip = sem("s_skip")
            s_att = sem("s_att")
            s_gv_ps = sem("s_gv_ps")
            s_a_att = sem("s_a_att")
            s_escale = sem("s_escale")
            s_mean = sem("s_mean")
            s_skip_add = sem("s_skip_add")
            s_x1 = sem("s_x1")

            SCANS = O * D // (P * 1024)
            SPB = SCANS // B
            assert SPB == 2
            w_pieces = w.rearrange("o (h d) -> (o h) d", d=1024).rearrange("(n p) d -> n p d", p=P)

            LAG = 7

            def piece(b, par, s, first):
                if first and s < LAG:
                    return None
                q, rest = divmod(s - LAG if s >= LAG else s - LAG + TPB, 2 * CT)
                return (b, par, q, rest // 2, rest % 2) if s >= LAG else (b - 1, 1 - par, q, rest // 2, rest % 2)

            GV = {9: 0, 10: 1, 11: 2, 12: 3}

            def batches(emit, eng):
                emit(0, 0, True, False)
                with eng.Fori(0, (B - 2) // 2) as i:
                    emit(2 * i + 1, 1, False, False)
                    emit(2 * i + 2, 0, False, False)
                emit(B - 1, (B - 1) % 2, False, True)

            with nc.Block() as block:

                @block.sync
                def _(sp):
                    def store_x1(b, par, q, ct, n):
                        sp.wait_ge(s_x1, n + 1)
                        sp.dma_start(x1_rows[b, :, ct, q * CH:(q + 1) * CH],
                                     xb[:, par, ct, q * CH:(q + 1) * CH]).then_inc(s_x1_stored[q], 16)

                    def load_x(b, par, q):
                        sp.dma_start(xb[:, par, :, q * CH:(q + 1) * CH], x_rows[b, :, :, q * CH:(q + 1) * CH]
                                     ).then_inc(s_x_in[par][q], 16)

                    for i, t in enumerate((wq, wk, wv, wskip)):
                        sp.dma_start(w_nat[:, i, :, :], t.rearrange("(t p) c -> p t c", p=P)
                                     ).then_inc(s_w_in[i // 2], 16)
                    sp.dma_start(ctxr[:, :, :], ctx_rows[0, :, :, :]).then_inc(s_ctx_in, 16)
                    sp.dma_start(gates[:, 0:1], g_xattn.rearrange("(a n) -> a n", a=1).to_broadcast([P, 1])
                                 ).then_inc(s_gates_in, 16)
                    sp.dma_start(gates[:, 1:2], g_ffn.rearrange("(a n) -> a n", a=1).to_broadcast([P, 1])
                                 ).then_inc(s_gates_in, 16)
                    for q in range(NQ):
                        load_x(0, 0, q)

                    def load_ffn_weights():
                        sp.dma_start(a_nat, lora_a.rearrange("n r d -> (n r) d")).then_inc(s_lora_in, 16)
                        for n in range(NADAPT):
                            sp.dma_start(coef[n * RANK:(n + 1) * RANK, :],
                                         lora_weights[n:n + 1].rearrange("(a n) -> a n", a=1).to_broadcast([RANK, 1])
                                         ).then_inc(s_lora_in, 16)
                        for n in range(NADAPT):
                            sp.dma_start(b_nat[:, :, n, :], lora_b[n].rearrange("(p t) r -> p t r", p=P)
                                         ).then_inc(s_lora_in, 16)
                        for blk in range(3):
                            load_w_block(sp, blk)
                        sp.dma_start(biasg[:, :], bias.rearrange("(a n) -> a n", a=1).to_broadcast([P, O])
                                     ).then_inc(s_bias_in, 16)

                    def emit(b, par, first, last):
                        if last:
                            load_ffn_weights()
                        else:
                            sp.wait_ge(s_ctxl, b + 1)
                            sp.dma_start(ctxr[:, :, :], ctx_rows[b + 1, :, :, :]).then_inc(s_ctx_in, 16)
                        for q in range(NQ):
                            if not first and q >= 2:
                                for ct in range(CT):
                                    store_x1(b - 1, 1 - par, q, ct, XPB * (b - 1) + CT * q + ct)
                            if not last:
                                if not first:
                                    sp.wait_ge(s_x1_stored[q], 16 * CT * b)
                                load_x(b + 1, 1 - par, q)
                        for q in range(2):
                            for ct in range(CT):
                                store_x1(b, par, q, ct, XPB * b + CT * q + ct)

                    batches(emit, sp)
                    for q in (2, 3):
                        for ct in range(CT):
                            store_x1(B - 1, (B - 1) % 2, q, ct, XPB * (B - 1) + CT * q + ct)
                    for q in range(NQ):
                        sp.wait_ge(s_x1_stored[q], 16 * CT * B)

                @block.gpsimd
                def _(pool):
                    nc.gpsimd.memset(ident[:, :], 0.0).then_inc(s_ident0, 1)
                    nc.gpsimd.memset(minus_half[:, :], -0.5).then_inc(s_half, 1)
                    pool.wait_ge(s_ident0, 1)
                    nc.gpsimd.affine_select(out=ident[:, :], in_=ident[:, :], compare_op=ALU.not_equal, fill=1.0,
                                            base=0, pattern=[[-1, P]], channel_multiplier=1).then_inc(s_ident, 1)
                    def rstd_of(b, par):
                        pool.wait_ge(s_vare, b + 1)
                        nc.gpsimd.tensor_tensor(rstd[:, par, :], vare[:, :], minus_half[:, 0:CT],
                                                ALU.pow).then_inc(s_rstd, 1)

                    def u_low(b, q):
                        for ct in range(CT):
                            pool.wait_ge(s_uh, 8 * b + 2 * q + ct + 1)
                            cols = slice(q * CH, (q + 1) * CH)
                            nc.gpsimd.tensor_tensor(ul[:, ct, cols], u32[:, ct, :], uh[:, ct, cols],
                                                    ALU.subtract).then_inc(s_ul, 1)

                    def ctx_max(b):
                        pool.wait_ge(s_cmax, b + 1)
                        nc.gpsimd.tensor_tensor(idle_pool[:, :], minus_half[:, 0:1], minus_half[:, 1:2], ALU.add)
                        nc.gpsimd.partition_all_reduce(cmaxa[:, :], cmax[:, :], P, RMAX).then_inc(s_cmaxa, 1)

                    pool.wait_ge(s_half, 1)
                    ctx_max(0)
                    pool.wait_ge(s_wmax, 3)
                    nc.gpsimd.partition_all_reduce(wmaxa[:, :], wmax[:, :], P, RMAX).then_inc(s_wmaxa, 1)
                    rstd_of(0, 0)
                    u_low(0, 0)
                    u_low(0, 1)

                    def emit(b, par, first, last):
                        if not last:
                            ctx_max(b + 1)
                        u_low(b, 2)
                        u_low(b, 3)
                        if not last:
                            rstd_of(b + 1, 1 - par)
                            u_low(b + 1, 0)
                            u_low(b + 1, 1)

                    batches(emit, pool)
                    pool.wait_ge(s_bias_in, 16)
                    pool.wait_ge(s_tanh, 1)
                    nc.gpsimd.tensor_scalar(biasg[:, :], biasg[:, :], tg[:, 1:2], None, ALU.mult)
                    pool.wait_ge(s_fmax, 3)
                    nc.gpsimd.partition_all_reduce(fmaxa[:, :], fmax[:, :], P, RMAX).then_inc(s_fmaxa, 1)

                @block.scalar
                def _(act):
                    act.wait_ge(s_gates_in, 32)
                    nc.scalar.activation(tg[:, :], gates[:, :], ACT.Tanh).then_inc(s_tanh, 1)

                    def ctx_high(b):
                        act.wait_ge(s_csc, 4 * b + 4)
                        nc.scalar.activation(ctxh[:, :, :], ctxr[:, :, :], ACT.Copy,
                                             scale=cscale[:, 0:1]).then_inc(s_ctxh, 1)

                    def gv_high(b, par, k):
                        act.wait_ge(s_gv_ps, 4 * b + k + 1)
                        dst = gh[:, par, k, :] if k < 2 else \
                            vh[:, par, 2 * k - 4:2 * k - 2, :].rearrange("p t c -> p (t c)")
                        nc.scalar.activation(dst, ps_gv[k][:, :], ACT.Copy, scale=2.0 ** GV_EXP).then_inc(s_gvh, 1)

                    def u_high(b, q, free):
                        if free is not None:
                            act.wait_ge(s_skip, free)
                        for ct in range(CT):
                            act.wait_ge(s_u32, 8 * b + 2 * q + ct + 1)
                            nc.scalar.activation(uh[:, ct, q * CH:(q + 1) * CH], u32[:, ct, :],
                                                 ACT.Copy).then_inc(s_uh, 1)

                    ctx_high(0)
                    act.wait_ge(s_wsc, 4)
                    for i in range(3):
                        nc.scalar.activation(wth[:, i, :, :].rearrange("p t c -> p (t c)"), ps_wt[i][:, :],
                                             ACT.Copy, scale=wscale[:, i:i + 1]).then_inc(s_wth, 1)
                    gv_high(0, 0, 0)
                    u_high(0, 0, None)
                    for k in range(1, 4):
                        gv_high(0, 0, k)
                    u_high(0, 1, None)

                    def exp_tile(b, par, s, first):
                        j = TPB * b + s
                        act.wait_ge(s_nbias, j + 1)
                        if not (first and s < 4):
                            act.wait_ge(s_t, j - 3)
                        nc.scalar.activation(pf[:, s % 4, :], ps_e[s % 2][:, :], ACT.Exp,
                                             bias=nbias[:, s % 4:s % 4 + 1], scale=e_scale[:, par:par + 1],
                                             accum_out=rsum[:, s % 4:s % 4 + 1]).then_inc(s_exp, 1)

                    def p_high(j, s):
                        act.wait_ge(s_t, j + 1)
                        nc.scalar.activation(pth[:, (s // TPC) % 2, :, (s % TPC) * P:(s % TPC + 1) * P],
                                             ps_t[s % 2][:, :].rearrange("p (t n) -> p t n", t=MT),
                                             ACT.Copy, scale=2.0 ** P_EXP).then_inc(s_pth, 1)

                    def p_normalise(j, s):
                        act.wait_ge(s_rinv, j + 1)
                        nc.scalar.activation(pf[:, s % 4, :], pf[:, s % 4, :], ACT.Copy,
                                             scale=rinv[:, s % 4:s % 4 + 1]).then_inc(s_pn, 1)

                    def load_piece(n, i):
                        act.dma_start(wscan[:, i, :], w_pieces[n, :, :]).then_inc(s_scan_in[i], 16)

                    def scan(b, i, final):
                        n = SPB * b + i
                        if not final:
                            if not (isinstance(n, int) and n == 0):
                                act.wait_ge(s_scanned, n)
                            load_piece(n + 1, 1 - i)
                        act.wait_ge(s_scan_in[i], 16 * (b + 1))
                        nc.scalar.activation(wjunk[:, :], wscan[:, i, :], ACT.Abs,
                                             accum_out=wabs[:, bass.ds(n, 1)]).then_inc(s_scanned, 1)

                    load_piece(0, 0)

                    def emit(b, par, first, last):
                        for s in range(TPB):
                            if not last and s - 1 in GV:
                                gv_high(b + 1, 1 - par, GV[s - 1])
                            exp_tile(b, par, s, first)
                            if not (first and s < 1):
                                p_normalise(TPB * b + s - 1, (s - 1) % TPB)
                            if not (first and s < 2):
                                p_high(TPB * b + s - 2, (s - 2) % TPB)
                            if s == 2:
                                u_high(b, 2, None if first else XPB * b - 2)
                            if s == 6:
                                u_high(b, 3, None if first else XPB * b)
                            if not last and s == 5:
                                ctx_high(b + 1)
                            if not last and s == 13:
                                u_high(b + 1, 0, XPB * b + 2)
                            if not last and s == 14:
                                u_high(b + 1, 1, XPB * b + 4)
                            if s in (4, 11):
                                scan(b, 0 if s == 4 else 1, last and s == 11)

                    batches(emit, act)
                    p_normalise(TPB * B - 1, TPB - 1)
                    for s in (TPB - 2, TPB - 1):
                        p_high(TPB * (B - 1) + s, s)

                @block.vector
                def _(dve):
                    def stats_of(b, par, q, ct):
                        if ct == 0:
                            dve.wait_ge(s_x_in[par][q], 8 * (b - par) + 16)
                        nc.vector.bn_stats(stats[:, ct, q, :], xb[:, par, ct, q * CH:(q + 1) * CH]
                                           ).then_inc(s_stats, 1)

                    def aggregate(b, par):
                        dve.wait_ge(s_stats, 8 * (b + 1))
                        nc.vector.tensor_copy(idle_dve[:, :], minus_half[:, 0:1])
                        for ct in range(CT):
                            nc.vector.bn_aggr(mv[:, ct, :], stats[:, ct, :, :].rearrange("p q s -> p (q s)")
                                              ).then_inc(s_aggr, 1)
                        dve.wait_ge(s_aggr, 2 * (b + 1))
                        nc.vector.tensor_copy(mean[:, par, :], mv[:, :, 0]).then_inc(s_mean, 1)
                        nc.vector.tensor_scalar(vare[:, :], mv[:, :, 1], EPS, 2.0 ** (-2 * U_EXP),
                                                ALU.add, ALU.mult).then_inc(s_vare, 1)

                    def normalise(b, par, q):
                        if q == 0:
                            dve.wait_ge(s_rstd, b + 1)
                            dve.wait_ge(s_mean, b + 1)
                        for ct in range(CT):
                            n = 8 * b + 2 * q + ct
                            if not (isinstance(n, int) and n < 2):
                                dve.wait_ge(s_ul, n - 1)
                            nc.vector.tensor_scalar(u32[:, ct, :], xb[:, par, ct, q * CH:(q + 1) * CH],
                                                    mean[:, par, ct:ct + 1], rstd[:, par, ct:ct + 1],
                                                    ALU.subtract, ALU.mult).then_inc(s_u32, 1)

                    def ctx_absmax(b):
                        dve.wait_ge(s_ctx_in, 16 * (b + 1))
                        nc.vector.tensor_reduce(cmax[:, :], ctxr[:, :, :], AX.XY, ALU.max,
                                                apply_absolute_value=True).then_inc(s_cmax, 1)

                    def power_of_two(dst, rec, scale, src, exponent, sem_, base):
                        nc.vector.tensor_scalar(rec, src, TINY, None, ALU.max).then_inc(sem_, 1)
                        dve.wait_ge(sem_, base + 1)
                        nc.vector.tensor_scalar(dst.bitcast(U32), rec.bitcast(U32), EXPONENT, None,
                                                ALU.bitwise_and).then_inc(sem_, 1)
                        dve.wait_ge(sem_, base + 2)
                        nc.vector.reciprocal(rec, dst).then_inc(sem_, 1)
                        dve.wait_ge(sem_, base + 3)
                        nc.vector.tensor_scalar(scale, rec, 2.0 ** exponent, None, ALU.mult).then_inc(sem_, 1)

                    def ctx_scale(b, par):
                        dve.wait_ge(s_cmaxa, b + 1)
                        power_of_two(cpow[:, :], crec[:, :], cscale[:, :], cmaxa[:, :], IN_EXP, s_csc, 4 * b)
                        nc.vector.tensor_tensor(e_scale[:, par:par + 1], cpow[:, :], c_exp[:, :], ALU.mult
                                                ).then_inc(s_escale, 1)

                    def attention_scale(b, par):
                        dve.wait_ge(s_csc, 4 * b + 2)
                        nc.vector.tensor_tensor(a_att[:, par:par + 1], cpow[:, :], c_att[:, :], ALU.mult
                                                ).then_inc(s_a_att, 1)

                    def ctx_low(b):
                        dve.wait_ge(s_ctxh, b + 1)
                        dve.wait_ge(s_csc, 4 * b + 4)
                        nc.vector.scalar_tensor_tensor(
                            out=ctxl[:, :, :].rearrange("p t m -> p (t m)"),
                            in0=ctxr[:, :, :].rearrange("p t m -> p (t m)"),
                            scalar=cscale[:, 0:1], in1=ctxh[:, :, :].rearrange("p t m -> p (t m)"),
                            op0=ALU.mult, op1=ALU.subtract).then_inc(s_ctxl, 1)

                    def gv_low(b, par, k):
                        dve.wait_ge(s_gvh, 4 * b + k + 1)
                        dst, hi = (gl[:, par, k, :], gh[:, par, k, :]) if k < 2 else \
                            (vl[:, par, 2 * k - 4:2 * k - 2, :].rearrange("p t c -> p (t c)"),
                             vh[:, par, 2 * k - 4:2 * k - 2, :].rearrange("p t c -> p (t c)"))
                        nc.vector.scalar_tensor_tensor(out=dst, in0=ps_gv[k][:, :], scalar=2.0 ** GV_EXP, in1=hi,
                                                       op0=ALU.mult, op1=ALU.subtract).then_inc(s_gv, 1)

                    def row_max(b, par, s):
                        j = TPB * b + s
                        dve.wait_ge(s_energy, j + 1)
                        nc.vector.tensor_reduce(nmax[:, s % 4:s % 4 + 1], ps_e[s % 2][:, :], AX.X, ALU.max,
                                                negate=True).then_inc(s_nmax, 1)
                        if s == 0:
                            dve.wait_ge(s_escale, b + 1)
                        dve.wait_ge(s_nmax, j + 1)
                        nc.vector.tensor_tensor(nbias[:, s % 4:s % 4 + 1], nmax[:, s % 4:s % 4 + 1],
                                                e_scale[:, par:par + 1], ALU.mult).then_inc(s_nbias, 1)

                    def row_sum(j, s):
                        dve.wait_ge(s_exp, j + 1)
                        nc.vector.reciprocal(rinv[:, s % 4:s % 4 + 1], rsum[:, s % 4:s % 4 + 1]).then_inc(s_rinv, 1)

                    def p_low(j, s):
                        dve.wait_ge(s_pth, j + 1)
                        cols = slice((s % TPC) * P, (s % TPC + 1) * P)
                        nc.vector.scalar_tensor_tensor(out=ptl[:, (s // TPC) % 2, :, cols],
                                                       in0=ps_t[s % 2][:, :].rearrange("p (t n) -> p t n", t=MT),
                                                       scalar=2.0 ** P_EXP, in1=pth[:, (s // TPC) % 2, :, cols],
                                                       op0=ALU.mult, op1=ALU.subtract).then_inc(s_ptl, 1)

                    def add_piece(what):
                        b, par, q, ct, is_att = what
                        x1 = xb[:, par, ct, q * CH:(q + 1) * CH]
                        n = XPB * b + CT * q + ct
                        if not is_att:
                            dve.wait_ge(s_skip, n + 1)
                            nc.vector.scalar_tensor_tensor(out=x1, in0=ps_s[ct][:, :], scalar=a_skip[:, 0:1],
                                                           in1=x1, op0=ALU.mult, op1=ALU.add).then_inc(s_skip_add, 1)
                        else:
                            dve.wait_ge(s_att, n + 1)
                            dve.wait_ge(s_skip_add, n + 1)
                            if q == 0 and ct == 0:
                                dve.wait_ge(s_a_att, b + 1)
                            nc.vector.scalar_tensor_tensor(out=x1, in0=ps_a[ct][:, :], scalar=a_att[:, par:par + 1],
                                                           in1=x1, op0=ALU.mult, op1=ALU.add).then_inc(s_x1, 1)

                    dve.wait_ge(s_half, 1)
                    ctx_absmax(0)
                    for i in range(3):
                        dve.wait_ge(s_wt_ps, i + 1)
                        nc.vector.tensor_reduce(wmax[:, i:i + 1], ps_wt[i][:, :], AX.X, ALU.max,
                                                apply_absolute_value=True).then_inc(s_wmax, 1)
                    dve.wait_ge(s_cmaxa, 1)
                    power_of_two(cpow[:, :], crec[:, :], cscale[:, :], cmaxa[:, :], IN_EXP, s_csc, 0)
                    dve.wait_ge(s_wmaxa, 1)
                    power_of_two(wpow[:, :], wrec[:, :], wscale[:, :], wmaxa[:, :], IN_EXP, s_wsc, 0)
                    for ct in range(CT):
                        stats_of(0, 0, 0, ct)
                    ctx_low(0)
                    dve.wait_ge(s_wsc, 4)
                    for i in range(3):
                        dve.wait_ge(s_wth, i + 1)
                        nc.vector.scalar_tensor_tensor(
                            out=wtl[:, i, :, :].rearrange("p t c -> p (t c)"),
                            in0=ps_wt[i][:, :], scalar=wscale[:, i:i + 1],
                            in1=wth[:, i, :, :].rearrange("p t c -> p (t c)"),
                            op0=ALU.mult, op1=ALU.subtract).then_inc(s_wtl, 1)
                    for q in range(1, NQ):
                        for ct in range(CT):
                            stats_of(0, 0, q, ct)
                    aggregate(0, 0)
                    nc.vector.tensor_scalar(c_exp[:, :], wpow[:, 0:1], 2.0 ** (-4 - U_EXP - GV_EXP - 2 * IN_EXP),
                                            None, ALU.mult).then_inc(s_wsc, 1)
                    dve.wait_ge(s_tanh, 1)
                    nc.vector.tensor_scalar(c_att[:, :], wpow[:, 1:2], tg[:, 0:1],
                                            2.0 ** (-P_EXP - GV_EXP - 2 * IN_EXP), ALU.mult, ALU.mult
                                            ).then_inc(s_wsc, 1)
                    nc.vector.tensor_scalar(a_skip[:, :], wpow[:, 2:3], tg[:, 0:1],
                                            2.0 ** (-U_EXP - IN_EXP), ALU.mult, ALU.mult).then_inc(s_wsc, 1)
                    gv_low(0, 0, 0)
                    normalise(0, 0, 0)
                    dve.wait_ge(s_wsc, 7)
                    nc.vector.tensor_tensor(e_scale[:, 0:1], cpow[:, :], c_exp[:, :], ALU.mult).then_inc(s_escale, 1)
                    attention_scale(0, 0)
                    for k in range(1, 4):
                        gv_low(0, 0, k)
                    normalise(0, 0, 1)

                    def emit(b, par, first, last):
                        for s in range(TPB):
                            j = TPB * b + s
                            if s - 1 in GV:
                                if last:
                                    bt_quarter(GV[s - 1])
                                else:
                                    gv_low(b + 1, 1 - par, GV[s - 1])
                            row_max(b, par, s)
                            if not (first and s < 1):
                                row_sum(j - 1, (s - 1) % TPB)
                            if not (first and s < 3):
                                p_low(j - 3, (s - 3) % TPB)
                            if s > 0 and piece(b, par, s - 1, first):
                                add_piece(piece(b, par, s - 1, first))
                            elif s == 0 and not first:
                                add_piece(piece(b - 1, 1 - par, TPB - 1, False))
                            if s == 2:
                                normalise(b, par, 2)
                            if s == 6:
                                normalise(b, par, 3)
                            if not last:
                                if s == 2:
                                    ctx_absmax(b + 1)
                                if s == 4:
                                    ctx_scale(b + 1, 1 - par)
                                if s == 5:
                                    ctx_low(b + 1)
                                if s == LAG + 1:
                                    attention_scale(b + 1, 1 - par)
                                if s in STATS:
                                    stats_of(b + 1, 1 - par, STATS[s], 0)
                                    stats_of(b + 1, 1 - par, STATS[s], 1)
                                if s == 12:
                                    aggregate(b + 1, 1 - par)
                                if s == 13:
                                    normalise(b + 1, 1 - par, 0)
                                if s == 14:
                                    normalise(b + 1, 1 - par, 1)
                            elif s == 5:
                                dve.wait_ge(s_lora_in, 16 * (1 + 2 * NADAPT))
                                max_of_lora(0, a_nat)
                            elif s == 14:
                                dve.wait_ge(s_gv, 4 * B + 4)
                                max_of_lora(1, bt[:, :])
                            elif s == 15:
                                dve.wait_ge(s_scanned, SCANS)
                                nc.vector.tensor_reduce(fmax[:, 2:3], wabs[:, :], AX.X, ALU.max).then_inc(s_fmax, 1)

                    def bt_quarter(k):
                        dve.wait_ge(s_gv_ps, 4 * B + k + 1)
                        nc.vector.tensor_scalar(
                            bt[:, :].rearrange("q (p t) -> q t p", t=KT)[:, 4 * k:4 * k + 4, :],
                            ps_gv[k][:, :].rearrange("q (t p) -> q t p", t=4), coef[:, 0:1], LORA_SCALE,
                            ALU.mult, ALU.mult).then_inc(s_gv, 1)

                    def max_of_lora(i, t):
                        nc.vector.tensor_reduce(fmax[:, i:i + 1], t, AX.X, ALU.max,
                                                apply_absolute_value=True).then_inc(s_fmax, 1)

                    def ffn_scale():
                        dve.wait_ge(s_fmaxa, 1)
                        nc.vector.tensor_tensor(fbound[:, 0:1], fmaxa[:, 0:1], fmaxa[:, 1:2], ALU.mult).then_inc(s_fsc, 1)
                        dve.wait_ge(s_fsc, 1)
                        nc.vector.scalar_tensor_tensor(out=fbound[:, 1:2], in0=fbound[:, 0:1], scalar=float(P),
                                                       in1=fmaxa[:, 2:3], op0=ALU.mult, op1=ALU.add).then_inc(s_fsc, 1)
                        dve.wait_ge(s_fsc, 2)
                        power_of_two(fpow[:, :], frec[:, :], fscale[:, :], fbound[:, 1:2], W_EXP, s_fsc, 2)
                        nc.vector.tensor_scalar(a_ffn[:, :], fpow[:, :], tg[:, 1:2], 2.0 ** (-U_EXP - W_EXP),
                                                ALU.mult, ALU.mult).then_inc(s_fsc, 1)

                    STATS = {3: 0, 6: 1, 9: 2, 11: 3}
                    batches(emit, dve)
                    row_sum(TPB * B - 1, TPB - 1)
                    for s in (TPB - 3, TPB - 2, TPB - 1):
                        p_low(TPB * (B - 1) + s, s)
                    add_piece(piece(B - 1, (B - 1) % 2, TPB - 1, False))
                    for s in range(LAG):
                        add_piece(piece(B, B % 2, s, False))
                        if s == 2:
                            ffn_scale()

                @block.tensor
                def _(pe):
                    def split_product(dst, terms, finish):
                        ops = [(lo_l if k == 2 else hi_l, lo_r if k == 1 else hi_r)
                               for (hi_l, lo_l), (hi_r, lo_r) in terms for k in range(3)]
                        for n, (lhs, rhs) in enumerate(ops):
                            ins = nc.tensor.matmul(dst, lhs, rhs, start=n == 0, stop=n == len(ops) - 1)
                        if finish is not None:
                            ins.then_inc(finish, 1)

                    pe.wait_ge(s_w_in[0], 32)
                    for k in range(CT):
                        for o in range(CT):
                            ins = nc.tensor.matmul(ps_wt[0][:, k * C:(k + 1) * C], w_nat[:, 1, o, k * P:(k + 1) * P],
                                                   w_nat[:, 0, o, :], start=o == 0, stop=o == CT - 1)
                    ins.then_inc(s_wt_ps, 1)
                    pe.wait_ge(s_ident, 1)
                    pe.wait_ge(s_w_in[1], 32)
                    for i in (1, 2):
                        for k in range(CT):
                            for o in range(CT):
                                ins = nc.tensor.transpose(ps_wt[i][:, k * C + o * P:k * C + (o + 1) * P],
                                                          w_nat[:, i + 1, o, k * P:(k + 1) * P], ident[:, :])
                        ins.then_inc(s_wt_ps, 1)

                    def g_or_v(b, par, k):
                        if k == 0:
                            pe.wait_ge(s_ctxl, b + 1)
                        if k < 2:
                            rows = slice(k * P, (k + 1) * P)
                            split_product(ps_gv[k][:, :],
                                          [((wth[:, 0, t, rows], wtl[:, 0, t, rows]), (ctxh[:, t, :], ctxl[:, t, :]))
                                           for t in range(CT)], s_gv_ps)
                        else:
                            for i in range(2):
                                rows = slice((2 * k - 4 + i) * P, (2 * k - 3 + i) * P)
                                split_product(ps_gv[k][:, i * C:(i + 1) * C],
                                              [((ctxh[:, t, rows], ctxl[:, t, rows]), (wth[:, 1, t, :], wtl[:, 1, t, :]))
                                               for t in range(CT)], s_gv_ps if i else None)

                    for k in range(4):
                        if k % 2 == 0:
                            pe.wait_ge(s_wtl, k // 2 + 1)
                        g_or_v(0, 0, k)
                    pe.wait_ge(s_wtl, 3)

                    def energy(b, par, s, first):
                        j = TPB * b + s
                        if s % TPC == 0:
                            pe.wait_ge(s_ul, 8 * b + 2 * (s // TPC) + 2)
                        if s == 0:
                            pe.wait_ge(s_gv, 4 * b + 2)
                        if not (first and s < 2):
                            pe.wait_ge(s_exp, j - 1)
                        split_product(ps_e[s % 2][:, :],
                                      [((uh[:, k, s * P:(s + 1) * P], ul[:, k, s * P:(s + 1) * P]),
                                        (gh[:, par, k, :], gl[:, par, k, :])) for k in range(CT)], s_energy)

                    def transpose_p(j, s):
                        pe.wait_ge(s_pn, j + 1)
                        if not (isinstance(j, int) and j < 2):
                            pe.wait_ge(s_ptl, j - 1)
                        for mt in range(MT):
                            ins = nc.tensor.transpose(ps_t[s % 2][:, mt * P:(mt + 1) * P],
                                                      pf[:, s % 4, mt * P:(mt + 1) * P], ident[:, :])
                        ins.then_inc(s_t, 1)

                    def transpose_lora_b(k):
                        if k == 0:
                            pe.wait_ge(s_lora_in, 16 * (1 + 2 * NADAPT))
                        for t in range(4):
                            ins = nc.tensor.transpose(ps_gv[k][:, t * P:(t + 1) * P],
                                                      b_nat[:, 4 * k + t, :, :].rearrange("p n r -> p (n r)"),
                                                      ident[:, :])
                        ins.then_inc(s_gv_ps, 1)

                    def sum_piece(what, first):
                        b, par, q, ct, is_att = what
                        n = XPB * b + CT * q + ct
                        cols = slice(q * CH, (q + 1) * CH)
                        rows = slice(ct * P, (ct + 1) * P)
                        k = 2 * ct + is_att
                        if q == 0 and first:
                            pe.wait_ge(s_gv, k + 1)
                        elif q == 1:
                            pe.wait_ge(s_gv, 4 * (b + 1) + k + 1)
                        else:
                            pe.wait_ge(s_x1 if is_att else s_skip_add, n - 1)
                        if not is_att:
                            split_product(ps_s[ct][:, :],
                                          [((wth[:, 2, t, rows], wtl[:, 2, t, rows]), (uh[:, t, cols], ul[:, t, cols]))
                                           for t in range(CT)], s_skip)
                            return
                        if ct == 0:
                            pe.wait_ge(s_ptl, TPB * b + TPC * (q + 1))
                            if q == 0:
                                pe.wait_ge(s_gv, 4 * b + 4)
                        split_product(ps_a[ct][:, :],
                                      [((vh[:, par, m, rows], vl[:, par, m, rows]),
                                        (pth[:, q % 2, m, :], ptl[:, q % 2, m, :])) for m in range(MT)], s_att)

                    def emit(b, par, first, last):
                        for s in range(TPB):
                            energy(b, par, s, first)
                            if s in GV:
                                k = GV[s]
                                pe.wait_ge(s_x1 if k % 2 else s_skip_add, XPB * b + k // 2 + 1)
                                if last:
                                    transpose_lora_b(k)
                                else:
                                    g_or_v(b + 1, 1 - par, k)
                            if piece(b, par, s, first):
                                sum_piece(piece(b, par, s, first), first)
                            if not (first and s < 2):
                                transpose_p(TPB * b + s - 2, (s - 2) % TPB)

                    batches(emit, pe)
                    for s in range(LAG):
                        sum_piece(piece(B, B % 2, s, False), False)
                        if s < 2:
                            transpose_p(TPB * B + s - 2, TPB + s - 2)

        with ExitStack() as phase:
            def sb(name, shape, dt):
                return phase.enter_context(nc.sbuf_tensor(name, shape, dt))

            def ps(name):
                return phase.enter_context(nc.psum_tensor(name, [P, CH], F32))

            wh = sb("wh", [P, OC * KT, CH], F16)
            wl = sb("wl", [P, OC * KT, CH], F16)
            u2t = sb("u2t", [P, 2, 2, KT, P], F16)
            stats2 = sb("stats2", [P, 4, 6], F32)
            mv2 = sb("mv2", [P, 2], F32)
            vare2 = sb("vare2", [P, 1], F32)
            rstd2 = sb("rstd2", [P, 1], F32)

            GROUPS = P // 32
            ps_w = [ps(f"ps_w{i}") for i in range(4)]
            ps_f = [ps(f"ps_f{i}") for i in range(OC)]

            w_stage.append(u2t[:, 1, :, :, :].rearrange("p h t n -> p (h t n)").bitcast(F32)
                           .rearrange("p (t d) -> p t d", t=4))

            def turned(r):
                return u2t[:, r % 2, :, :, :].rearrange("p h t n -> p (h t n)").bitcast(F32)

            s_unit = sem("s_unit")
            s_wh = sem("s_wh")
            s_wl = sem("s_wl")
            s_row_in = [sem(f"s_row_in{i}") for i in range(4)]
            s_out_stored = sem("s_out_stored")
            s_stats2 = sem("s_stats2")
            s_aggr2 = sem("s_aggr2")
            s_vare2 = sem("s_vare2")
            s_rstd2 = sem("s_rstd2")
            s_u2 = sem("s_u2")
            s_xbias = sem("s_xbias")
            s_turned = sem("s_turned")
            s_spread = sem("s_spread")
            s_u2h = sem("s_u2h")
            s_u2l = sem("s_u2l")
            s_f = sem("s_f")
            s_out = sem("s_out")

            def rows_part(k):
                return u2[:, :].rearrange("p (j t n) -> p t j n", j=GROUPS, t=KT)[:, 4 * k:4 * k + 4, :, :]

            def split_part(r, lo, k):
                return u2t[:, r % 2, lo, 4 * k:4 * k + 4, :].rearrange("p t (j n) -> p t j n", j=GROUPS)

            ROWS_AT = {13: (0,), 14: (1,), 15: (2, 3)}

            def row_tiles(emit, eng):
                for r in range(4):
                    emit(r, 0, r, r == 0, False)
                with eng.Fori(1, ST // 4 - 1) as i:
                    for r in range(4):
                        emit(4 * i + r, i, r, False, False)
                for r in range(4):
                    emit(ST - 4 + r, ST // 4 - 1, r, False, r == 3)

            with nc.Block() as block:

                @block.sync
                def _(sp):
                    def load_row(i, r):
                        sp.dma_start(xring[:, r, :], x1_tiles[i, :, :]).then_inc(s_row_in[r], 16)

                    def spread(i, r):
                        early = [(0, 0), (0, 1), (1, 0), (1, 1)]
                        for half in range(2):
                            sp.wait_ge(s_turned, 2 * i + half + 1)
                            for j, g in [(j, g) for j in range(GROUPS) for g in range(GROUPS)
                                         if ((j, g) in early) == (half == 0)]:
                                sp.dma_start(u2[g * 32:(g + 1) * 32, j * CH:(j + 1) * CH],
                                             turned(r)[j * 32:(j + 1) * 32, g * CH:(g + 1) * CH]
                                             ).then_inc(s_spread, 16)

                    load_w_block(sp, 3)
                    load_w_block(sp, 14)
                    for blk in range(4, 14):
                        sp.wait_ge(s_unit, 4 * (blk - 3))
                        load_w_block(sp, blk)
                    sp.wait_ge(s_unit, 4 * 11)
                    load_row(0, 0)
                    sp.wait_ge(s_unit, 4 * 13)
                    load_w_block(sp, 15)
                    spread(0, 0)
                    sp.wait_ge(s_unit, OC * KT)
                    load_row(1, 1)
                    load_row(2, 2)

                    def emit(i, f, r, first, last):
                        if not (isinstance(i, int) and i + 3 >= ST):
                            if not first:
                                sp.wait_ge(s_out_stored, 16 * i)
                            load_row(i + 3, (r + 3) % 4)
                        if not last:
                            spread(i + 1, r + 1)
                        if last:
                            for oc in range(OC):
                                sp.wait_ge(s_out, OC * i + oc + 1)
                                sp.dma_start(out_tiles[i, :, oc * CH:(oc + 1) * CH],
                                             xring[:, r, oc * CH:(oc + 1) * CH]).then_inc(s_out_stored, 16)
                        else:
                            sp.wait_ge(s_out, OC * (i + 1))
                            sp.dma_start(out_tiles[i, :, :], xring[:, r, :]).then_inc(s_out_stored, 16)

                    row_tiles(emit, sp)
                    sp.wait_ge(s_out_stored, 16 * (ST - 1 + OC))

                @block.gpsimd
                def _(pool):
                    def prepare(i, r):
                        pool.wait_ge(s_vare2, i + 1)
                        nc.gpsimd.tensor_tensor(rstd2[:, :], vare2[:, :], minus_half[:, 0:1],
                                                ALU.pow).then_inc(s_rstd2, 1)
                        pool.wait_ge(s_u2, i + 1)
                        nc.gpsimd.tensor_tensor(xring[:, r, :], xring[:, r, :], biasg[:, :],
                                                ALU.add).then_inc(s_xbias, 1)

                    def emit(i, f, r, first, last):
                        if not last:
                            prepare(i + 1, (r + 1) % 4)

                    prepare(0, 0)
                    row_tiles(emit, pool)

                @block.scalar
                def _(act):
                    def w_high(oc, kt):
                        act.wait_ge(s_unit, KT * oc + kt + 1)
                        nc.scalar.activation(wh[:, bass.ds(KT * oc + kt, 1), :], ps_w[kt % 4][:, None, :],
                                             ACT.Copy, scale=fscale[:, 0:1]).then_inc(s_wh, 1)

                    def u2_high(i, r, ks):
                        for k in ks:
                            if k == 0:
                                act.wait_ge(s_spread, 16 * GROUPS * GROUPS * (i + 1))
                            nc.scalar.activation(split_part(r, 0, k), rows_part(k), ACT.Copy).then_inc(s_u2h, 1)

                    def emit(i, f, r, first, last):
                        if not last:
                            u2_high(i + 1, r + 1, range(4))

                    with act.Fori(0, OC - 1) as oc:
                        for kt in range(KT):
                            w_high(oc, kt)
                    for kt in range(KT):
                        w_high(OC - 1, kt)
                        if kt in ROWS_AT:
                            u2_high(0, 0, ROWS_AT[kt])
                    row_tiles(emit, act)

                @block.vector
                def _(dve):
                    def row_stats(i, f, r, qs):
                        if qs[0] == 0:
                            dve.wait_ge(s_row_in[r], 16 * (f + 1))
                        for q in qs:
                            nc.vector.bn_stats(stats2[:, q, :], xring[:, r, q * CH:(q + 1) * CH]).then_inc(s_stats2, 1)

                    def row_aggregate(i):
                        dve.wait_ge(s_stats2, 4 * (i + 1))
                        nc.vector.tensor_copy(idle_dve[:, :], minus_half[:, 0:1])
                        nc.vector.bn_aggr(mv2[:, :], stats2[:, :, :].rearrange("p q s -> p (q s)")).then_inc(s_aggr2, 1)
                        dve.wait_ge(s_aggr2, i + 1)
                        nc.vector.tensor_scalar(vare2[:, :], mv2[:, 1:2], EPS, 2.0 ** (-2 * U_EXP),
                                                ALU.add, ALU.mult).then_inc(s_vare2, 1)

                    def row_normalise(i, r):
                        dve.wait_ge(s_rstd2, i + 1)
                        if isinstance(i, int) and i == 0:
                            dve.wait_ge(s_unit, KT * (OC - 1))
                        else:
                            dve.wait_ge(s_u2l, 4 * i)
                        nc.vector.tensor_scalar(
                            u2[:, :].rearrange("p (g t a) -> p t g a", g=GROUPS, t=KT),
                            xring[:, r, :].rearrange("p (t g a) -> p t g a", g=GROUPS, t=KT),
                            mv2[:, 0:1], rstd2[:, 0:1], ALU.subtract, ALU.mult).then_inc(s_u2, 1)

                    def row_turn(i, r, halves):
                        if halves[0] == 0:
                            dve.wait_ge(s_u2, i + 1)
                        if halves[0] == 0 and not (isinstance(i, int) and i < 2):
                            dve.wait_ge(s_f, OC * (i - 1))
                        for h in halves:
                            half = slice(h * D // 2, (h + 1) * D // 2)
                            nc.vector.transpose(turned(r)[:, half], u2[:, half]).then_inc(s_turned, 1)

                    def u2_low(i, r, ks):
                        for k in ks:
                            dve.wait_ge(s_u2h, 4 * i + k + 1)
                            nc.vector.tensor_tensor(split_part(r, 1, k), rows_part(k), split_part(r, 0, k),
                                                    ALU.subtract).then_inc(s_u2l, 1)

                    def finish(i, r, oc):
                        dve.wait_ge(s_f, OC * i + oc + 1)
                        if oc == 0:
                            dve.wait_ge(s_xbias, i + 1)
                        o = xring[:, r, oc * CH:(oc + 1) * CH]
                        nc.vector.scalar_tensor_tensor(out=o, in0=ps_f[oc][:, :], scalar=a_ffn[:, 0:1], in1=o,
                                                       op0=ALU.mult, op1=ALU.add).then_inc(s_out, 1)

                    def w_low(oc, kt):
                        dve.wait_ge(s_wh, KT * oc + kt + 1)
                        n = bass.ds(KT * oc + kt, 1)
                        nc.vector.scalar_tensor_tensor(
                            out=wl[:, n, :], in0=ps_w[kt % 4][:, None, :], scalar=fscale[:, 0:1],
                            in1=wh[:, n, :], op0=ALU.mult, op1=ALU.subtract).then_inc(s_wl, 1)

                    with dve.Fori(0, OC - 1) as oc:
                        for kt in range(KT):
                            w_low(oc, kt)
                    for kt in range(KT):
                        w_low(OC - 1, kt)
                        if kt < 2:
                            row_stats(0, 0, 0, (2 * kt, 2 * kt + 1))
                        if kt == 1:
                            row_aggregate(0)
                        if kt == 2:
                            row_normalise(0, 0)
                        if kt in (3, 5):
                            row_turn(0, 0, (kt // 2 - 1,))
                        if kt in ROWS_AT:
                            u2_low(0, 0, ROWS_AT[kt])

                    def emit(i, f, r, first, last):
                        if not last:
                            row_stats(i + 1, f + (1 if r == 3 else 0), (r + 1) % 4, range(4))
                            row_aggregate(i + 1)
                            row_normalise(i + 1, (r + 1) % 4)
                            row_turn(i + 1, r + 1, (0, 1))
                        finish(i, r, 0)
                        if not last:
                            u2_low(i + 1, r + 1, (0, 1))
                        finish(i, r, 1)
                        if not last:
                            u2_low(i + 1, r + 1, (2, 3))
                        finish(i, r, 2)
                        finish(i, r, 3)

                    row_tiles(emit, dve)

                @block.tensor
                def _(pe):
                    def unit(oc, kt):
                        stage = stage_of(4 * (OC - 1) + kt // 4) if isinstance(oc, int) and oc == OC - 1 else kt // 4
                        if kt % 4 == 0:
                            if isinstance(oc, int) and oc == OC - 1:
                                pe.wait_ge(s_wstage[stage], 16 * {12: 4, 13: 4, 14: 1, 15: 5}[12 + kt // 4])
                            else:
                                pe.wait_ge(s_wstage[stage], 16 * (oc + 1))
                        if not (isinstance(oc, int) and oc == 0 and kt < 4):
                            pe.wait_ge(s_wl, KT * oc + kt - 3)
                        for t in range(4):
                            nc.tensor.matmul(ps_w[kt % 4][:, t * P:(t + 1) * P],
                                             w_stage[stage][:, t, (kt % 4) * P:(kt % 4 + 1) * P],
                                             ident[:, :], is_transpose=True, start=t == 0, stop=False)
                        nc.tensor.matmul(ps_w[kt % 4][:, :], a_nat[:, kt * P:(kt + 1) * P],
                                         bt[:, bass.ds(CH * oc, CH)], start=False, stop=True).then_inc(s_unit, 1)

                    for kt in range(KT):
                        unit(0, kt)
                    with pe.Fori(1, OC - 1) as oc:
                        for kt in range(KT):
                            unit(oc, kt)

                    def product(i, r, oc):
                        if oc == 0 and not (isinstance(i, int) and i == 0):
                            pe.wait_ge(s_u2l, 4 * (i + 1))
                        if isinstance(i, int) and i == 0:
                            pe.wait_ge(s_wl, KT * (oc + 1))
                        if not (isinstance(i, int) and i == 0):
                            pe.wait_ge(s_out, OC * (i - 1) + oc + 1)
                        for kt in range(KT):
                            if oc == 0 and kt % 4 == 0 and isinstance(i, int) and i == 0:
                                pe.wait_ge(s_u2l, kt // 4 + 1)
                            hi, lo = u2t[:, r % 2, 0, kt, :], u2t[:, r % 2, 1, kt, :]
                            n = oc * KT + kt
                            nc.tensor.matmul(ps_f[oc][:, :], hi, wh[:, n, :], start=kt == 0, stop=False)
                            nc.tensor.matmul(ps_f[oc][:, :], hi, wl[:, n, :], start=False, stop=False)
                            ins = nc.tensor.matmul(ps_f[oc][:, :], lo, wh[:, n, :], start=False,
                                                   stop=kt == KT - 1)
                        ins.then_inc(s_f, 1)

                    for kt in range(KT):
                        unit(OC - 1, kt)

                    def emit(i, f, r, first, last):
                        for oc in range(OC):
                            product(i, r, oc)

                    row_tiles(emit, pe)


_INS = ["x", "ctx_1024", "g_xattn", "g_ffn", "L0_xattn_Wq", "L0_xattn_Wk", "L0_xattn_Wv", "L0_xattn_Wskip",
        "L0_ffn_lora_A", "L0_ffn_lora_B", "L0_ffn_W", "L0_ffn_bias", "L0_ffn_lora_weights"]


def kernel(**inputs):
    import numpy as _np
    import concourse.bacc as _bacc
    from concourse import mybir as _mybir
    from concourse.bass_utils import run_bass_kernel_spmd as _run

    nc = _bacc.Bacc("TRN2", target_bir_lowering=False, num_devices=1)
    arrays, args = {}, []
    for name in _INS:
        a = _np.ascontiguousarray(inputs[name])
        arrays[f"in_{name}"] = a
        args.append(nc.dram_tensor(f"in_{name}", a.shape, _mybir.dt.from_np(a.dtype), kind="ExternalInput").ap())
    args.append(nc.dram_tensor("out_0", inputs["x"].shape, _mybir.dt.float32, kind="ExternalOutput").ap())
    flamingo_kernel(nc, *args)
    r = _run(nc, [arrays], core_ids=[0])
    return r.results[0]["out_0"]
```
